# Optimizing a Trainium2 kernel written in Bass

```python
import numpy as np
import jax
import jax.numpy as jnp

def _softmax(x, axis=-1):
    return jax.nn.softmax(x, axis=axis)

def _gelu(x):
    return jax.nn.gelu(x, approximate=True)

def _silu(x):
    return jax.nn.silu(x)

def _sigmoid(x):
    return jax.nn.sigmoid(x)

def _layernorm(x, axis=-1, eps=1e-05):
    m = jnp.mean(x, axis=axis, keepdims=True)
    v = jnp.var(x, axis=axis, keepdims=True)
    return (x - m) / jnp.sqrt(v + eps)

def _scatter_add(tgt, idx, src, axis=0):
    return tgt.at[idx].add(src)

def _segment_sum(src, seg, n):
    return jax.ops.segment_sum(src, seg, n)
kernel_name = 'mk_seq_postln_d1_jaxref_r4_e854fa'

def setup_inputs(seed: int=0):
    np.random.seed(seed)
    _w = jnp.asarray

    def _L0_attn_setup():
        import jax, jax.numpy as jnp
        import numpy as np
        B, S, D = (2, 512, 256)
        H = 16
        HD = D // H

        def _rope_tables(seq_len, head_dim, dtype):
            pos = jnp.arange(seq_len, dtype=dtype)
            inv = jnp.power(10000.0, -2.0 * jnp.arange(head_dim // 2, dtype=dtype) / head_dim)
            ang = pos[:, None] * inv[None, :]
            cos_pos = jnp.repeat(jnp.cos(ang), 2, axis=-1)
            sin_pos = jnp.repeat(jnp.sin(ang), 2, axis=-1)
            return (cos_pos, sin_pos)

        def _rotate_half_interleaved(x):
            x2 = jnp.stack([-x[..., 1::2], x[..., 0::2]], axis=-1)
            return x2.reshape(x.shape)
        key = jax.random.key(seed)
        ks = jax.random.split(key, 4)
        scale = 1.0 / np.sqrt(D)
        return {'hidden_states': jax.random.normal(ks[0], (B, S, D), jnp.float32), 'Wq': jax.random.normal(ks[1], (D, D), jnp.float32) * scale, 'bq': jnp.zeros((D,), jnp.float32), 'Wk': jax.random.normal(ks[2], (D, D), jnp.float32) * scale, 'bk': jnp.zeros((D,), jnp.float32), 'Wv': jax.random.normal(ks[3], (D, D), jnp.float32) * scale, 'bv': jnp.zeros((D,), jnp.float32)}
    _L0_attn_in = _L0_attn_setup()

    def _L0_ffn_setup():
        import jax, jax.numpy as jnp
        import numpy as np
        DIM = 256

        def _reference_tuple_inner(x, W_r, W_k, W_v, mu_r, mu_k):
            B, T, C = x.shape
            x_prev = jnp.concatenate([jnp.zeros((B, 1, C), x.dtype), x[:, :-1, :]], axis=1)
            xr = mu_r * x + (1.0 - mu_r) * x_prev
            xk = mu_k * x + (1.0 - mu_k) * x_prev
            r = jax.nn.sigmoid(jnp.einsum('btc,dc->btd', xr, W_r))
            k = jnp.einsum('btc,dc->btd', xk, W_k)
            k_act = jnp.square(jax.nn.relu(k))
            out = r * jnp.einsum('btc,dc->btd', k_act, W_v)
            new_state = x[:, -1, :]
            return (out, new_state)
        key = jax.random.key(seed)
        ks = jax.random.split(key, 6)
        B, T, C = (8, 512, DIM)
        x = jax.random.normal(ks[0], (B, T, C), dtype=jnp.float32)
        s = 1.0 / np.sqrt(C)
        W_r = jax.random.uniform(ks[1], (C, C), jnp.float32, -s, s)
        W_k = jax.random.uniform(ks[2], (C, C), jnp.float32, -s, s)
        W_v = jax.random.uniform(ks[3], (C, C), jnp.float32, -s, s)
        mu_r = jax.random.uniform(ks[4], (C,), jnp.float32)
        mu_k = jax.random.uniform(ks[5], (C,), jnp.float32)
        return {'x': x, 'W_r': W_r, 'W_k': W_k, 'W_v': W_v, 'mu_r': mu_r, 'mu_k': mu_k}
    _L0_ffn_in = _L0_ffn_setup()
    _d = {'L0_attn_hidden_states': _L0_attn_in['hidden_states'], 'L0_attn_Wq': _L0_attn_in['Wq'], 'L0_attn_bq': _L0_attn_in['bq'], 'L0_attn_Wk': _L0_attn_in['Wk'], 'L0_attn_bk': _L0_attn_in['bk'], 'L0_attn_Wv': _L0_attn_in['Wv'], 'L0_attn_bv': _L0_attn_in['bv'], 'L0_ffn_W_r': _L0_ffn_in['W_r'], 'L0_ffn_W_k': _L0_ffn_in['W_k'], 'L0_ffn_W_v': _L0_ffn_in['W_v'], 'L0_ffn_mu_r': _L0_ffn_in['mu_r'], 'L0_ffn_mu_k': _L0_ffn_in['mu_k']}
    _x0 = _d['L0_attn_hidden_states']
    _d['L0_attn_hidden_states'] = jax.random.normal(jax.random.fold_in(jax.random.key(seed), 1), (2, 2048, 256), dtype=_x0.dtype)
    del _x0
    return _d

def reference(L0_attn_hidden_states, L0_attn_Wq, L0_attn_bq, L0_attn_Wk, L0_attn_bk, L0_attn_Wv, L0_attn_bv, L0_ffn_W_r, L0_ffn_W_k, L0_ffn_W_v, L0_ffn_mu_r, L0_ffn_mu_k):

    def _L0_attn_ref(hidden_states, Wq, bq, Wk, bk, Wv, bv):
        import jax, jax.numpy as jnp
        import numpy as np
        B, S, D = (2, 512, 256)
        H = 16
        HD = D // H

        def _rope_tables(seq_len, head_dim, dtype):
            pos = jnp.arange(seq_len, dtype=dtype)
            inv = jnp.power(10000.0, -2.0 * jnp.arange(head_dim // 2, dtype=dtype) / head_dim)
            ang = pos[:, None] * inv[None, :]
            cos_pos = jnp.repeat(jnp.cos(ang), 2, axis=-1)
            sin_pos = jnp.repeat(jnp.sin(ang), 2, axis=-1)
            return (cos_pos, sin_pos)

        def _rotate_half_interleaved(x):
            x2 = jnp.stack([-x[..., 1::2], x[..., 0::2]], axis=-1)
            return x2.reshape(x.shape)
        b, s, d = hidden_states.shape
        q = hidden_states @ Wq + bq
        k = hidden_states @ Wk + bk
        v = hidden_states @ Wv + bv
        q = q.reshape(b, s, H, HD).transpose(0, 2, 1, 3)
        k = k.reshape(b, s, H, HD).transpose(0, 2, 1, 3)
        v = v.reshape(b, s, H, HD).transpose(0, 2, 1, 3)
        cos_pos, sin_pos = _rope_tables(s, HD, hidden_states.dtype)
        q = q * cos_pos + _rotate_half_interleaved(q) * sin_pos
        k = k * cos_pos + _rotate_half_interleaved(k) * sin_pos
        scores = jnp.einsum('bhqd,bhkd->bhqk', q, k) / jnp.sqrt(jnp.asarray(HD, hidden_states.dtype))
        probs = jax.nn.softmax(scores, axis=-1)
        ctx = jnp.einsum('bhqk,bhkd->bhqd', probs, v)
        ctx = ctx.transpose(0, 2, 1, 3).reshape(b, s, d)
        return ctx

    def _L0_ffn_ref(x, W_r, W_k, W_v, mu_r, mu_k):
        import jax, jax.numpy as jnp
        import numpy as np
        DIM = 256

        def _reference_tuple_inner(x, W_r, W_k, W_v, mu_r, mu_k):
            B, T, C = x.shape
            x_prev = jnp.concatenate([jnp.zeros((B, 1, C), x.dtype), x[:, :-1, :]], axis=1)
            xr = mu_r * x + (1.0 - mu_r) * x_prev
            xk = mu_k * x + (1.0 - mu_k) * x_prev
            r = jax.nn.sigmoid(jnp.einsum('btc,dc->btd', xr, W_r))
            k = jnp.einsum('btc,dc->btd', xk, W_k)
            k_act = jnp.square(jax.nn.relu(k))
            out = r * jnp.einsum('btc,dc->btd', k_act, W_v)
            new_state = x[:, -1, :]
            return (out, new_state)
        return _reference_tuple_inner(x, W_r, W_k, W_v, mu_r, mu_k)[0]
    x = L0_attn_hidden_states
    x = _layernorm(x + _L0_attn_ref(x, L0_attn_Wq, L0_attn_bq, L0_attn_Wk, L0_attn_bk, L0_attn_Wv, L0_attn_bv), axis=-1)
    x = _layernorm(x + _L0_ffn_ref(x, L0_ffn_W_r, L0_ffn_W_k, L0_ffn_W_v, L0_ffn_mu_r, L0_ffn_mu_k), axis=-1)
    return x

_drawn_inputs = setup_inputs


def setup_inputs(seed=0):
    import zlib

    import numpy as np

    out = dict(_drawn_inputs(seed))
    spreads = {'L0_attn_bq': (0.0, 0.8), 'L0_attn_bk': (0.0, 0.8), 'L0_attn_bv': (0.0, 0.1)}
    factors = {'L0_ffn_W_r': 3.17, 'L0_ffn_mu_r': 6.415}
    for name, (base, spread) in spreads.items():
        noise = np.random.default_rng([zlib.crc32(name.encode()), seed]).standard_normal(out[name].shape)
        drawn = base * np.exp(spread * noise) if base else spread * noise
        out[name] = jnp.asarray(drawn.astype(out[name].dtype))
    for name, factor in factors.items():
        out[name] = (out[name] * factor).astype(out[name].dtype)
    return out
```

```python
from contextlib import ExitStack

import numpy as np

import concourse.bass as bass
from concourse import mybir

F32 = mybir.dt.float32
BF16 = mybir.dt.bfloat16
ALU = mybir.AluOpType
ACT = mybir.ActivationFunctionType
AX = mybir.AxisListType

BATCH, SEQ, DIM = 2, 2048, 256
HEADS, HEAD_DIM = 16, 16
PAIRS = HEAD_DIM // 2
P = 128
CHUNKS = DIM // P
TOK = 512
BLOCKS = SEQ // TOK
TILES = SEQ // P
TPB = TOK // P
ALL_HEADS = BATCH * HEADS
PARTS = 3
Q_PARTS = [0, 0, 0, 1, 1, 2]
K_PARTS = [0, 1, 2, 0, 1, 0]
BANDS = len(Q_PARTS)
ROWS = BANDS * HEAD_DIM
ROWS_M = ROWS + PARTS
VCOLS = 32
SCALE = float(HEAD_DIM) ** -0.5
EPS = 1e-5
DMA = 16

STACKS = 4
UNITS = TILES * BLOCKS
LOADS = 2 * BANDS
SCORE_CREDIT = 3
PV_CREDIT = 2
RING_CREDIT = 2
MAX_UNITS = 2 * TILES
RING_PER_HEAD = MAX_UNITS + 2
MAX_PLAN = [2, 2, 2, 3, 2, 3, 2, 3, 2, 3, 2, 3, 3, 0, 0, 0]
CTX_CYCLE = 2
LOOPS = ALL_HEADS // STACKS - 1
REGION = 26 * 1024
assert sum(MAX_PLAN) == MAX_UNITS and len(MAX_PLAN) == TILES


def score_bank(n):
    if n == UNITS - 1:
        return 1, 2
    return n % 3, 2 if n == 1 else 3


def build(nc, x_tok, x_ch, w_qk, b_qk, w_v, b_v, w_rkv, mu, cos_t, sin_t, ident, ident_h, out):
    parts_d = nc.dram_tensor("qk_parts", (PARTS, 2, 2, BATCH * P, SEQ), BF16, kind="Internal").ap()

    with ExitStack() as ctx:
        def sb(name, shape, dt=F32):
            return ctx.enter_context(nc.sbuf_tensor(name, shape, dt))

        def pb(name, shape):
            return ctx.enter_context(nc.psum_tensor(name, shape, F32))

        def sem(name):
            return ctx.enter_context(nc.semaphore(name))

        v_all = sb("v_all", [P, ALL_HEADS, TILES, HEAD_DIM])
        ctx_all = sb("ctx_all", [P, ALL_HEADS, TILES, HEAD_DIM])
        id32 = sb("id32", [P, P])
        id16 = sb("id16", [P, P], BF16)

        region = sb("region", [P, REGION])
        taken = [0]

        def cut(words, dt=F32):
            a = region[:, taken[0]:taken[0] + words]
            taken[0] += words
            return a if dt == F32 else a.bitcast(dt)

        w_qk_s = cut(CHUNKS * 4 * P).rearrange("p (c m) -> p c m", c=CHUNKS)
        w_v_s = cut(CHUNKS * DIM).rearrange("p (c n) -> p c n", c=CHUNKS)
        b_qk_s = cut(4)
        b_v_s = cut(DIM)
        cos_s = cut(SEQ)
        sin_s = cut(SEQ)
        x_blk = cut(2 * CHUNKS * TOK).rearrange("p (b c t) -> p b c t", b=2, c=CHUNKS)
        raw = cut(2 * 4 * TOK).rearrange("p (b i t) -> p b i t", b=2, i=4)
        e_cos, o_sin, o_cos, e_sin = (cut(2 * TOK).rearrange("p (s t) -> p s t", s=2) for _ in range(4))
        rot = cut(4 * TOK).rearrange("p (i t) -> p i t", i=4)
        rest = cut(4 * TOK).rearrange("p (i t) -> p i t", i=4)
        cuts = cut(2 * PARTS * 2 * TOK, BF16).rearrange("p (b a i t) -> p b a i t", b=2, a=PARTS, i=4)
        taken[0] = 0
        q_stack = cut(STACKS * SEQ // 2, BF16).rearrange("p (b t) -> p b t", b=STACKS)
        k_stack = cut(STACKS * SEQ // 2, BF16).rearrange("p (b t) -> p b t", b=STACKS)
        probs = cut(2 * BLOCKS * TOK).rearrange("p (g j t) -> p g j t", g=2, j=BLOCKS)
        v_aug = cut(2 * TILES * VCOLS).rearrange("p (b k c) -> p b k c", b=2, k=TILES)
        ctx_turn = cut(TOK)
        tile_max = cut(MAX_UNITS).rearrange("p (t c) -> p t c", c=2)
        neg_max = cut(TILES)
        neg_rest = cut(TILES)
        neg_cuts = cut(PARTS * TILES // 2, BF16).rearrange("p (a t) -> p a t", a=PARTS)
        neg_rows = cut(P // 2, BF16)
        recip = cut(TILES).rearrange("p (c j) -> p c j", c=TPB)
        taken[0] = REGION - BATCH * TILES * DIM
        z_all = cut(BATCH * TILES * DIM).rearrange("p (t d) -> p t d", d=DIM)
        taken[0] = 0
        w_rkv_s = cut(3 * CHUNKS * DIM).rearrange("p (w c n) -> p w c n", w=3, c=CHUNKS)
        mu_s = cut(2 * CHUNKS).rearrange("p (w c) -> p w c", w=2)
        mu_c = cut(2 * CHUNKS).rearrange("p (w c) -> p w c", w=2)
        stats = cut(BATCH * TILES * 6).rearrange("p (t s) -> p t s", s=6)
        moments = cut(BATCH * TILES * 2).rearrange("p (t s) -> p t s", s=2)
        std = cut(BATCH * TILES)
        rstd = cut(BATCH * TILES)
        eps_s = cut(1)
        y_blk = cut(2 * TPB * DIM).rearrange("p (b t d) -> p b t d", b=2, t=TPB)
        y_ch = cut(2 * CHUNKS * (TOK + 4)).rearrange("p (b c t) -> p b c t", b=2, c=CHUNKS)
        mixed = cut(2 * CHUNKS * TOK).rearrange("p (w c t) -> p w c t", w=2, c=CHUNKS)
        prev_part = cut(2 * CHUNKS * TOK).rearrange("p (w c t) -> p w c t", w=2, c=CHUNKS)
        gate = cut(TPB * DIM).rearrange("p (t d) -> p t d", t=TPB)
        relu = cut(CHUNKS * TOK).rearrange("p (c t) -> p c t", c=CHUNKS)
        key_act = cut(CHUNKS * TOK).rearrange("p (c t) -> p c t", c=CHUNKS)
        gated = cut(TPB * DIM).rearrange("p (t d) -> p t d", t=TPB)
        assert taken[0] <= REGION - BATCH * TILES * DIM

        score_ps = [pb(f"score_ps{i}", [P, TOK]) for i in range(3)]
        ring_ps = [pb(f"ring_ps{i}", [P, 2 * TOK]) for i in range(2)]
        pv_ps = pb("pv_ps", [P, TOK])

        weights_in = sem("weights_in")
        x_in = [sem(f"x_in{i}") for i in range(2)]
        qk_ready = sem("qk_ready")
        v_ready = sem("v_ready")
        raw_ready = sem("raw_ready")
        v_stored = sem("v_stored")
        dve_half = sem("dve_half")
        pool_half = sem("pool_half")
        rot_ready = sem("rot_ready")
        high_ready = sem("high_ready")
        rest_ready = sem("rest_ready")
        mid_ready = sem("mid_ready")
        low_ready = sem("low_ready")
        parts_out = [sem(f"parts_out{i}") for i in range(2)]
        stack_in = [sem(f"stack_in{i}") for i in range(STACKS)]
        ones_set = sem("ones_set")
        neg_in = [sem(f"neg_in{i}") for i in range(STACKS)]
        scores_ready = sem("scores_ready")
        exps_done = sem("exps_done")
        pv_done = sem("pv_done")
        pv_copied = sem("pv_copied")
        v_aug_ready = sem("v_aug_ready")
        ring_filled = sem("ring_filled")
        ring_freed = sem("ring_freed")
        neg_step = sem("neg_step")
        neg_cut = sem("neg_cut")
        recip_ready = sem("recip_ready")
        c_in = sem("c_in")
        c_small = sem("c_small")
        z_step = sem("z_step")
        stat_step = sem("stat_step")
        moments_ready = sem("moments_ready")
        std_ready = sem("std_ready")
        rstd_ready = sem("rstd_ready")
        y_ready = sem("y_ready")
        y_turned = sem("y_turned")
        y_ch_ready = sem("y_ch_ready")
        edge_ready = sem("edge_ready")
        prev_ready = sem("prev_ready")
        mixed_ready = sem("mixed_ready")
        r_ready = sem("r_ready")
        k_ready = sem("k_ready")
        gate_ready = sem("gate_ready")
        relu_ready = sem("relu_ready")
        key_ready = sem("key_ready")
        kv_ready = sem("kv_ready")
        gated_ready = sem("gated_ready")
        z2_ready = sem("z2_ready")
        out_ready = sem("out_ready")
        out_done = sem("out_done")

        block = ctx.enter_context(nc.Block())
        A_GROUPS = BATCH * BLOCKS

        def period_ops(first, last):
            unit = 0
            for kt in range(TILES):
                ops = []
                if kt == CTX_CYCLE and not first:
                    ops.append(("ctx", 0))
                if not last:
                    for _ in range(MAX_PLAN[kt]):
                        ops.append(("max", unit))
                        unit += 1
                    if kt == TILES - 1:
                        ops.append(("neg", 0))
                yield ops

        def ring_base(h):
            return MAX_UNITS + 1 + (h * RING_PER_HEAD - 1 if not isinstance(h, int) or h else 0)

        RING_TOTAL = ring_base(ALL_HEADS - 1) + 2

        def head(i, l):
            return i * STACKS + 1 + l, (1 + l) % STACKS

        def use(i, l, ahead=0):
            return i + (1 + l + ahead) // STACKS + 1

        @block.sync
        def _(sp):
            def load_x(first, t):
                par = t % 2
                sp.dma_start(x_blk[:, par], x_ch[:, :, bass.ds(first + t * TOK, TOK)].rearrange(
                    "c p t -> p c t")).then_inc(x_in[par], DMA)

            for i in range(2):
                sp.sem_inc(parts_out[i], DMA)
            with sp.Fori(0, BATCH) as b:
                first_token = sp.snap(b * SEQ)
                first_row = sp.snap(b * P)
                for t in range(BLOCKS):
                    sp.wait_ge(v_ready, 1 + b * BLOCKS * 2 + 2 * max(t - 1, 0))
                    load_x(first_token, t)
                for t in range(BLOCKS):
                    sp.wait_ge(low_ready, b * BLOCKS + t + 2)
                    for a in range(PARTS):
                        for eo in range(2):
                            for s in range(2):
                                sp.dma_start(parts_d[a, s, eo, bass.ds(first_row, P), t * TOK:(t + 1) * TOK],
                                             cuts[:, t % 2, a, 2 * eo + s, :]).then_inc(parts_out[t % 2], DMA)

            for i in range(2):
                sp.wait_ge(parts_out[i], DMA + DMA * PARTS * 4 * A_GROUPS // 2)

            def load_stacks(h, buf):
                for stack, s, which in ((q_stack, 0, Q_PARTS), (k_stack, 1, K_PARTS)):
                    for band, a in enumerate(which):
                        rows = slice(band * HEAD_DIM, (band + 1) * HEAD_DIM)
                        sp.dma_start(stack[rows, buf, :], parts_d[a, s, :, bass.ds(h * PAIRS, PAIRS), :])\
                            .then_inc(stack_in[buf], DMA)

            def load_neg(h, buf):
                sp.wait_ge(ring_freed, RING_CREDIT + ring_base(h))
                for a in range(PARTS):
                    sp.dma_start(q_stack[ROWS + a:ROWS + a + 1, buf, :],
                                 neg_rows[a * TILES:(a + 1) * TILES, :]).then_inc(neg_in[buf], DMA)

            sp.wait_ge(v_stored, 2 + 2 * A_GROUPS)
            sp.wait_ge(ones_set, 1)
            for h in range(STACKS):
                load_stacks(h, h)
            load_neg(0, 0)

            def period(i, l, last, refill):
                h, buf = head(i, l)
                if not last:
                    load_neg(h + 1, (buf + 1) % STACKS)
                if refill:
                    sp.wait_ge(scores_ready, (h + 1) * UNITS)
                    load_stacks(h + STACKS, buf)

            period(-1, STACKS - 1, False, True)
            sp.dma_start(z_all, x_tok.rearrange("(t p) d -> p t d", p=P)).then_inc(c_in, DMA)
            with sp.Fori(0, ALL_HEADS // STACKS - 2) as i:
                for l in range(STACKS):
                    period(i, l, False, True)
            for n in range(ALL_HEADS - STACKS - 4, ALL_HEADS - 1):
                period(n // STACKS, n % STACKS, n + 1 == ALL_HEADS - 1, n + 1 + STACKS < ALL_HEADS)

            sp.wait_ge(ring_freed, RING_CREDIT + RING_TOTAL)
            sp.dma_start(w_rkv_s, w_rkv.rearrange("w (c p) n -> p w c n", p=P)).then_inc(c_in, DMA)
            sp.dma_start(mu_s, mu).then_inc(c_in, DMA)
            out_t = out.rearrange("(t p) d -> p t d", p=P)
            for g in range(A_GROUPS):
                sp.wait_ge(out_ready, (g + 1) * TPB)
                sp.dma_start(out_t[:, g * TPB:(g + 1) * TPB, :], z_all[:, g * TPB:(g + 1) * TPB, :])\
                    .then_inc(out_done, DMA)
            sp.wait_ge(out_done, DMA * A_GROUPS)

        @block.tensor
        def _(pe):
            pe.sem_inc(pv_done, PV_CREDIT)
            pe.sem_inc(v_ready, 1)
            pe.wait_ge(weights_in, 8 * DMA)
            with pe.Fori(0, BATCH) as b:
                for t in range(BLOCKS):
                    par = t % 2
                    pe.wait_ge(x_in[par], (b * 2 + t // 2 + 1) * DMA)
                    for i in range(4):
                        pe.wait_ge(raw_ready, (b * BLOCKS + t) * 4 + i + 1)
                        o = ring_ps[i // 2][:, (i % 2) * TOK:(i % 2 + 1) * TOK]
                        for c in range(CHUNKS):
                            mm = pe.matmul(o, w_qk_s[:, c, i * P:(i + 1) * P], x_blk[:, par, c, :],
                                           start=c == 0, stop=c == CHUNKS - 1)
                        mm.then_inc(qk_ready, 1)
                    for half in range(2):
                        pe.wait_ge(v_stored, (b * BLOCKS + t) * 2 + half + 1)
                        for k in range(2):
                            lo = (2 * half + k) * P
                            for c in range(CHUNKS):
                                mm = pe.matmul(score_ps[half][:, k * DIM:(k + 1) * DIM],
                                               x_blk[:, par, c, lo:lo + P], w_v_s[:, c, :],
                                               start=c == 0, stop=c == CHUNKS - 1, skip_group_check=True)
                        mm.then_inc(v_ready, 1)

            def ring_op(kind, unit, k, buf):
                slot = ring_ps[slot_of[0]]
                slot_of[0] ^= 1
                pe.wait_ge(ring_freed, k + 1)
                if kind == "max":
                    qt, half = unit // 2, unit % 2
                    for c in range(2):
                        lo = (2 * half + c) * TOK
                        yield pe.matmul(slot[:, c * TOK:(c + 1) * TOK], q_stack[0:ROWS, buf, qt * P:(qt + 1) * P],
                                        k_stack[0:ROWS, buf, lo:lo + TOK], start=True, stop=True)
                elif kind == "neg":
                    yield neg_product(slot)
                else:
                    for c in range(TPB):
                        mm = pe.transpose(slot[:, c * P:(c + 1) * P], ctx_turn[:, c * P:(c + 1) * P], id32[:, :])
                    yield mm

            slot_of = [0]

            def neg_product(slot):
                return pe.matmul(slot[0:PARTS * TILES, 0:P], neg_cuts.rearrange("p a t -> p (a t)"), id16[:, :],
                                 start=True, stop=True)

            def pv(h, kt, buf2):
                for j in range(BLOCKS):
                    pe.wait_ge(exps_done, SCORE_CREDIT + h * UNITS + kt * BLOCKS + j + 1)
                    mm = pe.matmul(pv_ps[j * VCOLS:(j + 1) * VCOLS, :], v_aug[:, buf2, kt, :],
                                   probs[:, kt % 2, j, :], start=kt == 0, stop=kt == TILES - 1,
                                   skip_group_check=True)
                mm.then_inc(pv_done, 1)

            def period(i, l, first=False, last=False):
                h, buf = head(i, l)
                nbuf = (buf + 1) % STACKS
                k = ring_base(h)
                pe.wait_ge(neg_in[buf], use(i, l) * PARTS * DMA)
                for kt, ops in enumerate(period_ops(first, last)):
                    def products(k=k, ops=ops):
                        for n, (kind, unit) in enumerate(ops):
                            if kind == "max" and unit == 0:
                                pe.wait_ge(stack_in[nbuf], use(i, l, 1) * LOADS * DMA)
                            if kind == "neg":
                                pe.wait_ge(neg_cut, h + 2)
                            if kind == "ctx":
                                pe.wait_ge(pv_copied, h)
                            mm = None
                            for mm in ring_op(kind, unit, k + n, nbuf):
                                last_mm[0] = mm
                                if kind != "max":
                                    mm.then_inc(ring_filled, 1)
                                elif not halves[0]:
                                    halves[0] = 1
                                else:
                                    halves[0] = 0
                                    mm.then_inc(ring_filled, 1)
                                yield
                    halves, last_mm = [0], [None]
                    work = products()
                    k = k + len(ops)
                    for j in range(BLOCKS):
                        n = kt * BLOCKS + j
                        bank, back = score_bank(n)
                        pe.wait_ge(exps_done, SCORE_CREDIT + h * UNITS + n - back + 1)
                        pe.matmul(score_ps[bank][:, :], k_stack[0:ROWS_M, buf, kt * P:(kt + 1) * P],
                                  q_stack[0:ROWS_M, buf, j * TOK:(j + 1) * TOK],
                                  start=True, stop=True).then_inc(scores_ready, 1)
                        next(work, None)
                    for _ in work:
                        pass
                    if kt == 0:
                        if not first:
                            pv(h - 1, TILES - 1, (buf + 1) % 2)
                    else:
                        if kt == 1:
                            pe.wait_ge(v_aug_ready, h + 1)
                            if not first:
                                pe.wait_ge(pv_copied, h)
                        pv(h, kt - 1, buf % 2)

            pe.wait_ge(raw_ready, 4 * A_GROUPS + 4)
            pe.wait_ge(v_stored, 2 * A_GROUPS + 2)
            pe.wait_ge(stack_in[0], LOADS * DMA)
            for u in range(MAX_UNITS):
                for mm in ring_op("max", u, u, 0):
                    pass
                mm.then_inc(ring_filled, 1)
            pe.wait_ge(neg_cut, 1)
            for mm in ring_op("neg", 0, MAX_UNITS, 0):
                mm.then_inc(ring_filled, 1)

            period(-1, STACKS - 1, first=True)
            with pe.Fori(0, LOOPS) as i:
                for l in range(STACKS):
                    period(i, l)
            for l in range(STACKS - 1):
                period(LOOPS, l, last=l == STACKS - 2)
            pv(ALL_HEADS - 1, TILES - 1, (ALL_HEADS - 1) % 2)
            pe.wait_ge(pv_copied, ALL_HEADS)
            for mm in ring_op("ctx", 0, RING_TOTAL - 1, 0):
                mm.then_inc(ring_filled, 1)

            def turn(b, t):
                pe.wait_ge(y_ready, b * BLOCKS + t + 1)
                pe.wait_ge(y_ch_ready, b * BLOCKS + t + 1)
                for c in range(CHUNKS):
                    for n in range(TPB):
                        mm = pe.transpose(score_ps[c][:, n * P:(n + 1) * P],
                                          y_blk[:, t % 2, n, c * P:(c + 1) * P], id32[:, :])
                mm.then_inc(y_turned, 1)

            pe.wait_ge(c_in, 3 * DMA)
            pe.wait_ge(ring_freed, RING_CREDIT + RING_TOTAL)
            with pe.Fori(0, BATCH) as b:
                turn(b, 0)
                for t in range(BLOCKS):
                    n = b * BLOCKS + t
                    pe.wait_ge(mixed_ready, n + 2)
                    pe.wait_ge(gate_ready, n + 1)
                    for q in range(TPB):
                        for c in range(CHUNKS):
                            mm = pe.matmul(ring_ps[0][:, q * DIM:(q + 1) * DIM], mixed[:, 0, c, q * P:(q + 1) * P],
                                           w_rkv_s[:, 0, c, :], start=c == 0, stop=c == CHUNKS - 1,
                                           skip_group_check=True)
                    mm.then_inc(r_ready, 1)
                    pe.wait_ge(relu_ready, n + 1)
                    for m, o in enumerate((score_ps[2], pv_ps)):
                        for c in range(CHUNKS):
                            mm = pe.matmul(o[:, :], w_rkv_s[:, 1, c, m * P:(m + 1) * P], mixed[:, 1, c, :],
                                           start=c == 0, stop=c == CHUNKS - 1)
                    mm.then_inc(k_ready, 1)
                    if t + 1 < BLOCKS:
                        turn(b, t + 1)
                    pe.wait_ge(key_ready, n + 2)
                    pe.wait_ge(gated_ready, n + 1)
                    for q in range(TPB):
                        for c in range(CHUNKS):
                            mm = pe.matmul(ring_ps[1][:, q * DIM:(q + 1) * DIM], key_act[:, c, q * P:(q + 1) * P],
                                           w_rkv_s[:, 2, c, :], start=c == 0, stop=c == CHUNKS - 1,
                                           skip_group_check=True)
                    mm.then_inc(kv_ready, 1)

        @block.scalar
        def _(act):
            n_in = 0
            for dst, src in ((w_qk_s, w_qk.rearrange("(c p) m -> p c m", p=P)),
                             (w_v_s, w_v.rearrange("(c p) n -> p c n", p=P)),
                             (b_qk_s, b_qk), (b_v_s, b_v.partition_broadcast(P)),
                             (cos_s, cos_t), (sin_s, sin_t), (id32[:, :], ident), (id16[:, :], ident_h)):
                act.dma_start(dst, src).then_inc(weights_in, DMA)
                n_in += 1
            assert n_in == 8
            act.sem_inc(raw_ready, 4)
            act.wait_ge(weights_in, 8 * DMA)

            def evacuate(b, t):
                for i in range(4):
                    act.wait_ge(qk_ready, (b * BLOCKS + t) * 4 + i + 1)
                    if i == 0:
                        act.wait_ge(rot_ready, b * BLOCKS + t + 1)
                    act.activation(raw[:, t % 2, i, :], ring_ps[i // 2][:, (i % 2) * TOK:(i % 2 + 1) * TOK],
                                   ACT.Identity, bias=b_qk_s[:, i:i + 1]).then_inc(raw_ready, 1)

            with act.Fori(0, BATCH) as b:
                for t in range(BLOCKS):
                    evacuate(b, t)
                    n = b * BLOCKS + t
                    act.wait_ge(rot_ready, n + 3)
                    act.wait_ge(parts_out[t % 2], DMA + (b * 2 + t // 2) * DMA * PARTS * 4)
                    act.activation(cuts[:, t % 2, 0], rot, ACT.Copy).then_inc(high_ready, 1)
                    act.wait_ge(rest_ready, n + 1)
                    act.activation(cuts[:, t % 2, 1], rest, ACT.Copy).then_inc(mid_ready, 1)

            act.sem_inc(exps_done, SCORE_CREDIT)

            def period(i, l, first=False):
                h, _ = head(i, l)
                for kt in range(TILES):
                    if kt == 1 and not first:
                        copy_pv(h)
                    act.wait_ge(pv_done, h * TILES + kt + 1)
                    for j in range(BLOCKS):
                        n = kt * BLOCKS + j
                        act.wait_ge(scores_ready, h * UNITS + n + 1)
                        act.activation(probs[:, kt % 2, j, :], score_ps[score_bank(n)[0]][:, :], ACT.Exp,
                                       scale=SCALE).then_inc(exps_done, 1)

            def copy_pv(h):
                act.wait_ge(pv_done, PV_CREDIT + h * TILES)
                if not isinstance(h, int) or h > 1:
                    act.wait_ge(recip_ready, h)
                act.copy(ctx_turn, pv_ps[:, :]).then_inc(pv_copied, 1)

            period(-1, STACKS - 1, first=True)
            with act.Fori(0, LOOPS) as i:
                for l in range(STACKS):
                    period(i, l)
            for l in range(STACKS - 1):
                period(LOOPS, l)
            copy_pv(ALL_HEADS)

            def std_of(n):
                act.wait_ge(moments_ready, n)
                act.activation(std, moments[:, :, 1], ACT.Sqrt, bias=eps_s).then_inc(std_ready, 1)

            act.wait_ge(c_in, 3 * DMA)
            act.wait_ge(c_small, 1)
            std_of(BATCH * TILES)
            act.sem_inc(y_ch_ready, 1)
            act.sem_inc(gate_ready, 1)
            act.sem_inc(relu_ready, 1)

            def take_turned(b, t):
                n = b * BLOCKS + t
                act.wait_ge(y_turned, n + 1)
                act.wait_ge(mixed_ready, n + 1)
                for c in range(CHUNKS):
                    ins = act.copy(y_ch[:, t % 2, c, 1:TOK + 1], score_ps[c][:, :])
                ins.then_inc(y_ch_ready, 1)
                act.wait_ge(edge_ready, n + 1)
                act.wait_ge(y_ch_ready, n + 2)
                for w in range(2):
                    for c in range(CHUNKS):
                        ins = act.mul(prev_part[:, w, c, :], y_ch[:, t % 2, c, 0:TOK], mu_c[:, w, c:c + 1])
                ins.then_inc(prev_ready, 1)

            with act.Fori(0, BATCH) as b:
                take_turned(b, 0)
                for t in range(BLOCKS):
                    n = b * BLOCKS + t
                    act.wait_ge(r_ready, n + 1)
                    act.wait_ge(gated_ready, n + 1)
                    act.activation(gate.rearrange("p t d -> p (t d)"), ring_ps[0][:, :], ACT.Sigmoid)\
                        .then_inc(gate_ready, 1)
                    act.wait_ge(k_ready, n + 1)
                    act.wait_ge(key_ready, n + 1)
                    for c, o in enumerate((score_ps[2], pv_ps)):
                        ins = act.activation(relu[:, c, :], o[:, :], ACT.Relu)
                    ins.then_inc(relu_ready, 1)
                    if t + 1 < BLOCKS:
                        take_turned(b, t + 1)
            std_of(2 * BATCH * TILES)

        @block.gpsimd
        def _(pool):
            pool.wait_ge(weights_in, 8 * DMA)

            def both(a):
                return a.unsqueeze(1).broadcast_to([P, 2, TOK])

            with pool.Fori(0, BATCH) as b:
                for t in range(BLOCKS):
                    n = b * BLOCKS + t
                    sin_b = both(sin_s[:, t * TOK:(t + 1) * TOK])
                    pool.wait_ge(raw_ready, 4 + 4 * n + 4)
                    pool.wait_ge(rot_ready, n + 2)
                    pool.tensor_tensor(o_sin, raw[:, t % 2, 2:4, :], sin_b, ALU.mult)
                    pool.tensor_tensor(e_sin, raw[:, t % 2, 0:2, :], sin_b, ALU.mult).then_inc(pool_half, 1)
                    pool.wait_ge(high_ready, n + 1)
                    pool.wait_ge(low_ready, n + 1)
                    pool.tensor_tensor(rest, rot, cuts[:, t % 2, 0], ALU.subtract).then_inc(rest_ready, 1)

            def lay_v(h, buf2, waits):
                if waits:
                    pool.wait_ge(pv_done, PV_CREDIT + (h - 1) * TILES)
                pool.tensor_copy(v_aug[:, buf2, :, 0:HEAD_DIM], v_all[:, h]).then_inc(v_aug_ready, 1)

            pool.wait_ge(ones_set, 1)
            pool.wait_ge(v_stored, 2 + 2 * A_GROUPS)
            lay_v(0, 0, False)
            lay_v(1, 1, False)
            with pool.Fori(0, (ALL_HEADS - 2) // 2) as i:
                for l in range(2):
                    lay_v(i * 2 + 2 + l, l, True)

        @block.vector
        def _(dve):
            def both(a):
                return a.unsqueeze(1).broadcast_to([P, 2, TOK])

            dve.sem_inc(rot_ready, 2)
            dve.sem_inc(v_stored, 2)
            dve.sem_inc(low_ready, 1)
            dve.sem_inc(recip_ready, 1)
            dve.wait_ge(weights_in, 8 * DMA)
            with dve.Fori(0, BATCH) as b:
                for t in range(BLOCKS):
                    n = b * BLOCKS + t
                    cos_b = both(cos_s[:, t * TOK:(t + 1) * TOK])
                    dve.wait_ge(raw_ready, 4 + 4 * n + 4)
                    dve.tensor_tensor(o_cos, raw[:, t % 2, 2:4, :], cos_b, ALU.mult)
                    dve.tensor_tensor(e_cos, raw[:, t % 2, 0:2, :], cos_b, ALU.mult).then_inc(dve_half, 1)
                    dve.wait_ge(pool_half, n + 1)
                    dve.wait_ge(dve_half, n + 1)
                    dve.wait_ge(low_ready, n + 1)
                    dve.tensor_tensor(rot[:, 2:4], o_cos, e_sin, ALU.add)
                    dve.tensor_tensor(rot[:, 0:2], e_cos, o_sin, ALU.subtract).then_inc(rot_ready, 1)
                    for half in range(2):
                        dve.wait_ge(v_ready, 2 * n + half + 2)
                        for k in range(2):
                            tile = TPB * t + 2 * half + k
                            ins = dve.tensor_tensor(
                                v_all[:, bass.ds(b * HEADS, HEADS), tile, :],
                                score_ps[half][:, k * DIM:(k + 1) * DIM].rearrange("p (h d) -> p h d", d=HEAD_DIM),
                                b_v_s.rearrange("p (h d) -> p h d", d=HEAD_DIM), ALU.add)
                        ins.then_inc(v_stored, 1)
                    dve.wait_ge(mid_ready, n + 1)
                    dve.tensor_tensor(cuts[:, t % 2, 2], rest, cuts[:, t % 2, 1], ALU.subtract)\
                        .then_inc(low_ready, 1)

            for i in range(2):
                dve.wait_ge(parts_out[i], DMA + DMA * PARTS * 4 * A_GROUPS // 2)
            dve.wait_ge(low_ready, 1 + A_GROUPS)
            dve.memset(k_stack[ROWS:ROWS_M, :, :], 1.0)
            dve.memset(v_aug[:, :, :, HEAD_DIM:HEAD_DIM + 1], 1.0)
            dve.memset(v_aug[:, :, :, HEAD_DIM + 1:VCOLS], 0.0).then_inc(ones_set, 1)
            dve.sem_inc(ring_freed, RING_CREDIT)

            slot_of = [0]

            def ring_read(kind, unit, k, h, before=None):
                slot = ring_ps[slot_of[0]]
                slot_of[0] ^= 1
                if kind == "neg":
                    cut_maxima(h)
                dve.wait_ge(ring_filled, k + 1)
                if kind == "max":
                    dve.reduce_max(tile_max[:, unit // 2, unit % 2:unit % 2 + 1], slot[:, :], AX.X)\
                        .then_inc(ring_freed, 1)
                elif kind == "neg":
                    if before is not None:
                        dve.wait_ge(neg_in[before[0]], before[1] * PARTS * DMA)
                    dve.tensor_copy(neg_rows[0:PARTS * TILES, :], slot[0:PARTS * TILES, 0:P])\
                        .then_inc(ring_freed, 1)
                else:
                    dve.wait_ge(ring_freed, RING_CREDIT + k)
                    turned = slot[:, 0:TOK].rearrange("p (c j v) -> p c j v", c=TPB, j=BLOCKS)
                    dve.reciprocal(recip, turned[:, :, :, HEAD_DIM]).then_inc(recip_ready, 1)
                    dve.wait_ge(recip_ready, h + 2)
                    o = ctx_all[:, h].rearrange("p (j c) d -> p c j d", c=TPB)
                    dve.tensor_tensor(o, turned[:, :, :, 0:HEAD_DIM],
                                      recip.unsqueeze(3).broadcast_to([P, TPB, BLOCKS, HEAD_DIM]), ALU.mult)\
                        .then_inc(ring_freed, 1)

            def cut_maxima(h):
                dve.wait_ge(ring_freed, RING_CREDIT + neg_at[0])
                dve.tensor_reduce(neg_max, tile_max, AX.X, ALU.max, negate=True).then_inc(neg_step, 1)
                dve.wait_ge(neg_step, h * 4 + 1)
                dve.tensor_copy(neg_cuts[:, 0, :], neg_max).then_inc(neg_step, 1)
                dve.wait_ge(neg_step, h * 4 + 2)
                dve.tensor_tensor(neg_rest, neg_max, neg_cuts[:, 0, :], ALU.subtract).then_inc(neg_step, 1)
                dve.wait_ge(neg_step, h * 4 + 3)
                dve.tensor_copy(neg_cuts[:, 1, :], neg_rest).then_inc(neg_step, 1)
                dve.wait_ge(neg_step, h * 4 + 4)
                dve.tensor_tensor(neg_cuts[:, 2, :], neg_rest, neg_cuts[:, 1, :], ALU.subtract)\
                    .then_inc(neg_cut, 1)

            neg_at = [MAX_UNITS]
            for u in range(MAX_UNITS):
                ring_read("max", u, u, 0)
            ring_read("neg", 0, MAX_UNITS, 0)

            def period(i, l, first=False, last=False):
                h, buf = head(i, l)
                k = ring_base(h)
                for kt, ops in enumerate(period_ops(first, last)):
                    for kind, unit in ops:
                        neg_at[0] = k
                        ring_read(kind, unit, k, h - 1 if kind == "ctx" else h + 1, (buf, use(i, l)))
                        k = k + 1

            period(-1, STACKS - 1, first=True)
            with dve.Fori(0, LOOPS) as i:
                for l in range(STACKS):
                    period(i, l)
            for l in range(STACKS - 1):
                period(LOOPS, l, last=l == STACKS - 2)
            ring_read("ctx", 0, RING_TOTAL - 1, ALL_HEADS - 1)

            dve.wait_ge(ring_freed, RING_CREDIT + RING_TOTAL)
            dve.wait_ge(c_in, 3 * DMA)
            dve.memset(eps_s, EPS)
            dve.tensor_scalar(mu_c, mu_s, -1.0, 1.0, ALU.mult, ALU.add).then_inc(c_small, 1)
            for b in range(BATCH):
                for t in range(TILES):
                    tile = b * TILES + t
                    o = z_all[:, tile, :].rearrange("p (h d) -> p h d", d=HEAD_DIM)
                    dve.tensor_tensor(o, o, ctx_all[:, b * HEADS:(b + 1) * HEADS, t, :], ALU.add)\
                        .then_inc(z_step, 1)

            def tile_stats(tile, count):
                dve.bn_stats(stats[:, tile, :], z_all[:, tile, :]).then_inc(stat_step, 1)
                dve.wait_ge(stat_step, count)
                dve.bn_aggr(moments[:, tile, :], stats[:, tile, :]).then_inc(moments_ready, 1)

            for tile in range(BATCH * TILES):
                dve.wait_ge(z_step, tile + 1)
                tile_stats(tile, tile + 1)
            dve.wait_ge(std_ready, 1)
            dve.reciprocal(rstd, std).then_inc(rstd_ready, 1)
            dve.wait_ge(rstd_ready, 1)
            dve.sem_inc(gated_ready, 1)
            dve.sem_inc(mixed_ready, 1)
            dve.sem_inc(key_ready, 1)

            def normalise(b, t):
                n = b * BLOCKS + t
                if n >= 2:
                    dve.wait_ge(y_turned, n - 1)
                for q in range(TPB):
                    tile = b * TILES + t * TPB + q
                    ins = dve.tensor_scalar(y_blk[:, t % 2, q, :], z_all[:, tile, :], moments[:, tile, 0:1],
                                            rstd[:, tile:tile + 1], ALU.subtract, ALU.mult)
                ins.then_inc(y_ready, 1)

            def mix(b, t):
                n = b * BLOCKS + t
                if t == 0:
                    dve.wait_ge(y_ch_ready, n + 1)
                    dve.memset(y_ch[:, 0, :, 0:1], 0.0).then_inc(edge_ready, 1)
                else:
                    dve.wait_ge(y_ch_ready, n + 1)
                    dve.tensor_copy(y_ch[:, t % 2, :, 0:1], y_ch[:, (t + 1) % 2, :, TOK:TOK + 1])\
                        .then_inc(edge_ready, 1)
                dve.wait_ge(prev_ready, n + 1)
                dve.wait_ge(k_ready, n)
                for w in range(2):
                    for c in range(CHUNKS):
                        ins = dve.scalar_tensor_tensor(mixed[:, w, c, :], y_ch[:, t % 2, c, 1:TOK + 1],
                                                       mu_s[:, w, c:c + 1], prev_part[:, w, c, :],
                                                       ALU.mult, ALU.add)
                ins.then_inc(mixed_ready, 1)

            for b in range(BATCH):
                normalise(b, 0)
                mix(b, 0)
                for t in range(BLOCKS):
                    n = b * BLOCKS + t
                    if t + 1 < BLOCKS:
                        normalise(b, t + 1)
                    dve.wait_ge(relu_ready, n + 2)
                    dve.wait_ge(kv_ready, n)
                    dve.tensor_tensor(key_act, relu, relu, ALU.mult).then_inc(key_ready, 1)
                    if t + 1 < BLOCKS:
                        mix(b, t + 1)
                    dve.wait_ge(kv_ready, n + 1)
                    dve.wait_ge(gate_ready, n + 2)
                    flat = gated.rearrange("p t d -> p (t d)")
                    dve.tensor_tensor(flat, ring_ps[1][:, :], gate.rearrange("p t d -> p (t d)"), ALU.mult)\
                        .then_inc(gated_ready, 1)
                    dve.wait_ge(gated_ready, n + 2)
                    dve.tensor_tensor(z_all[:, n * TPB:(n + 1) * TPB, :], gated, y_blk[:, t % 2], ALU.add)\
                        .then_inc(z2_ready, 1)
                    dve.wait_ge(z2_ready, n + 1)
                    for q in range(TPB):
                        tile_stats(n * TPB + q, BATCH * TILES + n * TPB + q + 1)
            dve.wait_ge(std_ready, 2)
            dve.reciprocal(rstd, std).then_inc(rstd_ready, 1)
            dve.wait_ge(rstd_ready, 2)
            for tile in range(BATCH * TILES):
                dve.tensor_scalar(z_all[:, tile, :], z_all[:, tile, :], moments[:, tile, 0:1],
                                  rstd[:, tile:tile + 1], ALU.subtract, ALU.mult).then_inc(out_ready, 1)


def rotary_tables():
    inv = np.power(np.float32(10000.0), np.float32(-2.0) * np.arange(PAIRS, dtype=np.float32) / np.float32(HEAD_DIM))
    ang = np.arange(SEQ, dtype=np.float32)[None, :] * inv.astype(np.float32)[:, None]
    return (np.tile(np.cos(ang).astype(np.float32), (HEADS, 1)), np.tile(np.sin(ang).astype(np.float32), (HEADS, 1)))


def kernel(**inputs):
    import concourse.bacc as bacc
    from concourse.bass_utils import run_bass_kernel_spmd
    import ml_dtypes

    x = np.asarray(inputs["L0_attn_hidden_states"]).reshape(BATCH * SEQ, DIM)
    wq, wk, wv = (np.asarray(inputs[f"L0_attn_W{n}"]) for n in "qkv")
    bq, bk, bv = (np.asarray(inputs[f"L0_attn_b{n}"]) for n in "qkv")
    even, odd = np.arange(0, DIM, 2), np.arange(1, DIM, 2)
    cos_t, sin_t = rotary_tables()
    arrays = {
        "x_tok": x,
        "x_ch": np.ascontiguousarray(x.T).reshape(CHUNKS, P, BATCH * SEQ),
        "w_qk": np.concatenate([wq[:, even], wk[:, even], wq[:, odd], wk[:, odd]], axis=1),
        "b_qk": np.stack([bq[even], bk[even], bq[odd], bk[odd]], axis=1),
        "w_v": wv,
        "b_v": bv,
        "w_rkv": np.stack([np.asarray(inputs[f"L0_ffn_W_{n}"]).T for n in "rkv"]),
        "mu": np.stack([np.asarray(inputs[f"L0_ffn_mu_{n}"]).reshape(CHUNKS, P) for n in "rk"]).transpose(2, 0, 1),
        "cos_t": cos_t,
        "sin_t": sin_t,
        "ident": np.eye(P, dtype=np.float32),
        "ident_h": np.eye(P, dtype=ml_dtypes.bfloat16),
    }
    arrays = {n: np.ascontiguousarray(a) for n, a in arrays.items()}
    nc = bacc.Bacc("TRN2", target_bir_lowering=False, num_devices=1)
    args = [nc.dram_tensor(n, a.shape, mybir.dt.from_np(a.dtype), kind="ExternalInput").ap()
            for n, a in arrays.items()]
    out = nc.dram_tensor("out", (BATCH * SEQ, DIM), F32, kind="ExternalOutput").ap()
    build(nc, *args, out)
    r = run_bass_kernel_spmd(nc, [arrays], core_ids=[0])
    return r.results[0]["out"].reshape(BATCH, SEQ, DIM)
```

```python
from contextlib import ExitStack

import numpy as np

import concourse.bass as bass
from concourse import mybir

F32 = mybir.dt.float32
BF16 = mybir.dt.bfloat16
ALU = mybir.AluOpType
ACT = mybir.ActivationFunctionType
AX = mybir.AxisListType

BATCH, SEQ, DIM = 2, 2048, 256
HEADS, HEAD_DIM = 16, 16
PAIRS = HEAD_DIM // 2
P = 128
CHUNKS = DIM // P
TOK = 512
BLOCKS = SEQ // TOK
TILES = SEQ // P
TPB = TOK // P
ALL_HEADS = BATCH * HEADS
PARTS = 3
Q_BANDS = [(0, 3), (1, 2), (2, 1)]
K_BANDS = [(0, 3), (0, 2), (0, 1)]
BANDS = sum(n for _, n in Q_BANDS)
ROWS = BANDS * HEAD_DIM
ROWS_M = ROWS + PARTS
VCOLS = 32
SCALE = float(HEAD_DIM) ** -0.5
EPS = 1e-5
DMA = 16

STACKS = 4
UNITS = TILES * BLOCKS
LOADS = len(Q_BANDS) + len(K_BANDS)
SCORE_CREDIT = 3
PV_CREDIT = 2
RING_CREDIT = 2
MAX_UNITS = 2 * TILES
RING_PER_HEAD = MAX_UNITS + 2
LEAD = 3
EARLY = 2 * LEAD
NEG_CYCLE = TILES - LEAD
CTX_CYCLE = 2
LOOPS = ALL_HEADS // STACKS - 1
EARLY_OUT = 6
REGION = 23 * 1024


def score_bank(n):
    if n == UNITS - 1:
        return 1, 2
    return n % 3, 2 if n == 1 else 3


def build(nc, x_tok, x_ch, w_qk, b_qk, w_v, b_v, w_rkv, mu, cos_t, sin_t, ident, ident_h, out):
    parts_d = nc.dram_tensor("qk_parts", (BATCH * P, 2, PARTS, 2, SEQ), BF16, kind="Internal").ap()

    with ExitStack() as ctx:
        def sb(name, shape, dt=F32):
            return ctx.enter_context(nc.sbuf_tensor(name, shape, dt))

        def pb(name, shape):
            return ctx.enter_context(nc.psum_tensor(name, shape, F32))

        def sem(name):
            return ctx.enter_context(nc.semaphore(name))

        v_all = sb("v_all", [P, ALL_HEADS, TILES, HEAD_DIM])
        ctx_all = sb("ctx_all", [P, ALL_HEADS, TILES, HEAD_DIM])
        id32 = sb("id32", [P, P])
        id16 = sb("id16", [P, P], BF16)
        q_stack = sb("q_stack", [P, STACKS, SEQ], BF16)
        k_stack = sb("k_stack", [P, STACKS, SEQ], BF16)
        v_aug = sb("v_aug", [P, 2, TILES, VCOLS])

        region = sb("region", [P, REGION])
        taken = [0]

        def cut(words, dt=F32):
            a = region[:, taken[0]:taken[0] + words]
            taken[0] += words
            return a if dt == F32 else a.bitcast(dt)

        w_qk_s = cut(CHUNKS * 4 * P).rearrange("p (c m) -> p c m", c=CHUNKS)
        w_v_s = cut(CHUNKS * DIM).rearrange("p (c n) -> p c n", c=CHUNKS)
        b_qk_s = cut(4)
        b_v_s = cut(DIM)
        cos_s = cut(SEQ)
        sin_s = cut(SEQ)
        x_blk = cut(2 * CHUNKS * TOK).rearrange("p (b c t) -> p b c t", b=2, c=CHUNKS)
        raw = cut(2 * 4 * TOK).rearrange("p (b i t) -> p b i t", b=2, i=4)
        e_cos, o_sin, o_cos, e_sin = (cut(2 * TOK).rearrange("p (s t) -> p s t", s=2) for _ in range(4))
        free = ctx_all[:, :, :, :].rearrange("p h t d -> p (h t d)").rearrange("p (w b e s t) -> p w b e s t", w=2, b=2, e=2, s=2)
        rot, rest = free[:, 0], free[:, 1]
        cuts = cut(2 * PARTS * 2 * TOK, BF16).rearrange("p (b e a s t) -> p b e a s t", b=2, e=2, a=PARTS, s=2)
        taken[0] = 0
        probs = cut(2 * BLOCKS * TOK).rearrange("p (g j t) -> p g j t", g=2, j=BLOCKS)
        ctx_turn = cut(TOK)
        tile_max = cut(MAX_UNITS).rearrange("p (t c) -> p t c", c=2)
        neg_max = cut(TILES)
        neg_rest = cut(TILES)
        neg_cuts = cut(PARTS * TILES // 2, BF16).rearrange("p (a t) -> p a t", a=PARTS)
        neg_rows = cut(P // 2, BF16)
        recip = cut(TILES).rearrange("p (c j) -> p c j", c=TPB)
        taken[0] = REGION - BATCH * TILES * DIM
        z_all = cut(BATCH * TILES * DIM).rearrange("p (t b d) -> p t b d", b=BATCH, d=DIM)
        taken[0] = 0
        w_rkv_s = cut(3 * CHUNKS * DIM).rearrange("p (w c n) -> p w c n", w=3, c=CHUNKS)
        mu_s = cut(2 * CHUNKS).rearrange("p (w c) -> p w c", w=2)
        mu_c = cut(2 * CHUNKS).rearrange("p (w c) -> p w c", w=2)
        stats = cut(BATCH * TILES * 6).rearrange("p (t s) -> p t s", s=6)
        moments = cut(BATCH * TILES * 2).rearrange("p (t s) -> p t s", s=2)
        std = cut(BATCH * TILES)
        rstd = cut(BATCH * TILES)
        eps_s = cut(1)
        y_ch = cut(2 * CHUNKS * (TOK + 4)).rearrange("p (b c t) -> p b c t", b=2, c=CHUNKS)
        mixed = cut(2 * CHUNKS * TOK).rearrange("p (w c t) -> p w c t", w=2, c=CHUNKS)
        prev_part = cut(2 * CHUNKS * TOK).rearrange("p (w c t) -> p w c t", w=2, c=CHUNKS)
        free = v_all[:, :, :, :].rearrange("p h t d -> p (h t d)")
        y_blk = free[:, 0:3 * TPB * DIM].rearrange("p (b t d) -> p b t d", b=3, t=TPB)
        relu = free[:, 3 * TPB * DIM:4 * TPB * DIM].rearrange("p (c t) -> p c t", c=CHUNKS)
        gate = free[:, 4 * TPB * DIM:6 * TPB * DIM].rearrange("p (b t d) -> p b t d", b=2, t=TPB)
        key_act = free[:, 6 * TPB * DIM:8 * TPB * DIM].rearrange("p (b c t) -> p b c t", b=2, c=CHUNKS)
        gated = cut(TPB * DIM).rearrange("p (t d) -> p t d", t=TPB)
        assert taken[0] <= REGION - BATCH * TILES * DIM

        score_ps = [pb(f"score_ps{i}", [P, TOK]) for i in range(3)]
        ring_ps = [pb(f"ring_ps{i}", [P, 2 * TOK]) for i in range(2)]
        pv_ps = pb("pv_ps", [P, TOK])

        weights_in = sem("weights_in")
        x_in = [sem(f"x_in{i}") for i in range(2)]
        qk_ready = sem("qk_ready")
        v_ready = sem("v_ready")
        raw_ready = sem("raw_ready")
        v_stored = sem("v_stored")
        products = sem("products")
        pool_product = sem("pool_product")
        rot_ready = sem("rot_ready")
        high_ready = sem("high_ready")
        rest_ready = sem("rest_ready")
        mid_ready = sem("mid_ready")
        low_ready = sem("low_ready")
        parts_out = [sem(f"parts_out{i}") for i in range(2)]
        stack_in = [sem(f"stack_in{i}") for i in range(STACKS)]
        ones_set = sem("ones_set")
        neg_in = [sem(f"neg_in{i}") for i in range(STACKS)]
        scores_ready = sem("scores_ready")
        exps_done = sem("exps_done")
        pv_done = sem("pv_done")
        pv_copied = sem("pv_copied")
        v_aug_ready = sem("v_aug_ready")
        ring_filled = sem("ring_filled")
        ring_freed = sem("ring_freed")
        neg_step = sem("neg_step")
        neg_cut = sem("neg_cut")
        recip_ready = sem("recip_ready")
        x_tok_in = sem("x_tok_in")
        z_ready = sem("z_ready")
        c_in = sem("c_in")
        c_small = sem("c_small")
        stat_step = sem("stat_step")
        moments_ready = sem("moments_ready")
        std_ready = sem("std_ready")
        rstd_ready = sem("rstd_ready")
        y_ready = sem("y_ready")
        y_turned = sem("y_turned")
        y_ch_ready = sem("y_ch_ready")
        edge_ready = sem("edge_ready")
        prev_ready = sem("prev_ready")
        mixed_ready = sem("mixed_ready")
        r_ready = sem("r_ready")
        k_ready = sem("k_ready")
        gate_ready = sem("gate_ready")
        relu_ready = sem("relu_ready")
        key_ready = sem("key_ready")
        kv_ready = sem("kv_ready")
        gated_ready = sem("gated_ready")
        z2_ready = sem("z2_ready")
        out_ready = sem("out_ready")
        out_done = sem("out_done")

        block = ctx.enter_context(nc.Block())
        A_GROUPS = BATCH * BLOCKS

        def after(eng, signal, count):
            if count > 0:
                eng.wait_ge(signal, count)

        def z_tile(tile):
            return z_all[:, tile % TILES, tile // TILES, :]

        def z_block(n):
            t = n % BLOCKS * TPB
            return z_all[:, t:t + TPB, n // BLOCKS, :]

        def period_ops(first=False, heads_after=2):
            for kt in range(TILES):
                ops = []
                if kt == CTX_CYCLE and not first:
                    ops.append(("ctx", -1, 0))
                for u in (2 * kt, 2 * kt + 1):
                    if u + EARLY < MAX_UNITS:
                        if heads_after >= 1:
                            ops.append(("max", 1, u + EARLY))
                            if u + EARLY == MAX_UNITS - 1:
                                ops.append(("cut", 1, 0))
                    elif heads_after >= 2:
                        ops.append(("max", 2, u + EARLY - MAX_UNITS))
                if kt == NEG_CYCLE and heads_after >= 1:
                    ops.append(("neg", 1, 0))
                yield ops

        OPENING = [("max", 0, u) for u in range(MAX_UNITS)] + [("cut", 0, 0)]
        OPENING += [("max", 1, 0), ("max", 1, 1), ("neg", 0, 0)] + [("max", 1, u) for u in range(2, EARLY)]

        def ring_len(ops):
            return sum(kind != "cut" for kind, _, _ in ops)

        def ring_base(h):
            if isinstance(h, int) and h == 0:
                return ring_len(OPENING)
            if isinstance(h, int) and h == ALL_HEADS - 1:
                return ring_base(h - 1) + RING_PER_HEAD - EARLY
            return ring_len(OPENING) + h * RING_PER_HEAD - 1

        def ctx_read(h):
            if isinstance(h, int) and h >= ALL_HEADS - 2:
                return RING_TOTAL - (ALL_HEADS - 1 - h)
            return ring_base(h + 1) + 2 * CTX_CYCLE + 1

        def neg_read(h):
            known = isinstance(h, int)
            at = [op for ops in period_ops(known and h == 0, min(2, ALL_HEADS - 1 - h) if known else 2)
                  for op in ops]
            return ring_base(h) + ring_len(at[:at.index(("neg", 1, 0)) + 1])

        RING_TOTAL = ring_base(ALL_HEADS - 1) + 2

        def head(i, l):
            return i * STACKS + 1 + l, (1 + l) % STACKS

        def use(i, l, ahead=0):
            return i + (1 + l + ahead) // STACKS + 1

        @block.sync
        def _(sp):
            def load_x(n):
                after(sp, v_ready, 2 * (n - 1))
                sp.dma_start(x_blk[:, n % 2], x_ch[:, :, n * TOK:(n + 1) * TOK].rearrange("c p t -> p c t"))\
                    .then_inc(x_in[n % 2], DMA)

            def store_parts(n):
                b, t = n // BLOCKS, n % BLOCKS
                sp.wait_ge(low_ready, n + 1)
                sp.dma_start(parts_d[b * P:(b + 1) * P, :, :, :, t * TOK:(t + 1) * TOK].rearrange(
                    "r e a s t -> r (e a s) t"), cuts[:, n % 2].rearrange("p e a s t -> p (e a s) t"))\
                    .then_inc(parts_out[n % 2], DMA)

            def load_stacks(h, buf):
                band = 0
                for a, reps in Q_BANDS:
                    src = parts_d[bass.ds(h * PAIRS, PAIRS), :, a, 0, :].rearrange("i e t -> (i e) t")
                    sp.dma_start(q_stack[band * HEAD_DIM:(band + reps) * HEAD_DIM, buf, :],
                                 src.unsqueeze(0).broadcast_to([reps, HEAD_DIM, SEQ])).then_inc(stack_in[buf], DMA)
                    band += reps
                band = 0
                for a, reps in K_BANDS:
                    src = parts_d[bass.ds(h * PAIRS, PAIRS), :, a:a + reps, 1, :]
                    sp.dma_start(k_stack[band * HEAD_DIM:(band + reps) * HEAD_DIM, buf, :],
                                 src.rearrange("i e a t -> a (i e) t")).then_inc(stack_in[buf], DMA)
                    band += reps

            def load_neg(reads, buf):
                sp.wait_ge(ring_freed, RING_CREDIT + reads)
                for a in range(PARTS):
                    sp.dma_start(q_stack[ROWS + a:ROWS + a + 1, buf, :],
                                 neg_rows[a * TILES:(a + 1) * TILES, :]).then_inc(neg_in[buf], DMA)

            load_x(0)
            load_x(1)
            load_x(2)
            for n in range(A_GROUPS):
                if n + 3 < A_GROUPS:
                    load_x(n + 3)
                store_parts(n)
                if n == A_GROUPS - 2:
                    for i in range(2):
                        sp.wait_ge(parts_out[i], DMA * BLOCKS // 2)
                    for h in range(STACKS):
                        load_stacks(h, h)
            sp.wait_ge(v_stored, 2 * A_GROUPS)
            for i in range(2):
                sp.wait_ge(parts_out[i], DMA * A_GROUPS // 2)
            for b in range(BATCH):
                sp.dma_start(z_all[:, :, b, :], x_tok[b * SEQ:(b + 1) * SEQ, :].rearrange("(t p) d -> p t d", p=P))\
                    .then_inc(x_tok_in, DMA)
            load_neg(ring_len(OPENING[:OPENING.index(("neg", 0, 0)) + 1]), 0)

            def period(i, l, refill=True, last=False):
                h, buf = head(i, l)
                if not last:
                    load_neg(neg_read(h), (buf + 1) % STACKS)
                if refill:
                    sp.wait_ge(scores_ready, (h + 1) * UNITS)
                    load_stacks(h + STACKS, buf)

            period(-1, STACKS - 1)
            with sp.Fori(0, LOOPS - 1) as i:
                for l in range(STACKS):
                    period(i, l)
            for n in range((LOOPS - 1) * STACKS, ALL_HEADS - 1):
                period(n // STACKS, n % STACKS, n + 1 + STACKS < ALL_HEADS, n + 1 == ALL_HEADS - 1)

            sp.wait_ge(ring_freed, RING_CREDIT + RING_TOTAL)
            sp.dma_start(w_rkv_s, w_rkv.rearrange("w (c p) n -> p w c n", p=P)).then_inc(c_in, DMA)
            sp.dma_start(mu_s, mu).then_inc(c_in, DMA)
            out_t = out.rearrange("(t p) d -> p t d", p=P)
            for g in range(A_GROUPS):
                sp.wait_ge(out_ready, (g + 1) * TPB)
                sp.dma_start(out_t[:, g * TPB:(g + 1) * TPB, :], z_block(g))\
                    .then_inc(out_done, DMA)
            sp.wait_ge(out_done, DMA * A_GROUPS)

        @block.tensor
        def _(pe):
            pe.sem_inc(pv_done, PV_CREDIT)
            pe.wait_ge(weights_in, 8 * DMA)
            for n in range(A_GROUPS):
                par = n % 2
                pe.wait_ge(x_in[par], (n // 2 + 1) * DMA)
                for i in range(4):
                    after(pe, raw_ready, 4 * (n - 1) + i + 1)
                    o = ring_ps[i // 2][:, (i % 2) * TOK:(i % 2 + 1) * TOK]
                    for c in range(CHUNKS):
                        mm = pe.matmul(o, w_qk_s[:, c, i * P:(i + 1) * P], x_blk[:, par, c, :],
                                       start=c == 0, stop=c == CHUNKS - 1)
                    mm.then_inc(qk_ready, 1)
                for half in range(2):
                    after(pe, v_stored, 2 * (n - 1) + half + 1)
                    for k in range(2):
                        lo = (2 * half + k) * P
                        for c in range(CHUNKS):
                            mm = pe.matmul(score_ps[half][:, k * DIM:(k + 1) * DIM],
                                           x_blk[:, par, c, lo:lo + P], w_v_s[:, c, :],
                                           start=c == 0, stop=c == CHUNKS - 1, skip_group_check=True)
                    mm.then_inc(v_ready, 1)

            def ring_op(kind, unit, k, buf):
                slot = ring_ps[slot_of[0]]
                slot_of[0] ^= 1
                pe.wait_ge(ring_freed, k + 1)
                if kind == "max":
                    qt, half = unit // 2, unit % 2
                    for c in range(2):
                        lo = (2 * half + c) * TOK
                        yield pe.matmul(slot[:, c * TOK:(c + 1) * TOK], q_stack[0:ROWS, buf, qt * P:(qt + 1) * P],
                                        k_stack[0:ROWS, buf, lo:lo + TOK], start=True, stop=True)
                elif kind == "neg":
                    yield neg_product(slot)
                else:
                    for c in range(TPB):
                        mm = pe.transpose(slot[:, c * P:(c + 1) * P], ctx_turn[:, c * P:(c + 1) * P], id32[:, :])
                    yield mm

            slot_of = [0]

            def neg_product(slot):
                return pe.matmul(slot[0:PARTS * TILES, 0:P], neg_cuts.rearrange("p a t -> p (a t)"), id16[:, :],
                                 start=True, stop=True)

            def pv(h, kt, buf2):
                for j in range(BLOCKS):
                    pe.wait_ge(exps_done, SCORE_CREDIT + h * UNITS + kt * BLOCKS + j + 1)
                    mm = pe.matmul(pv_ps[j * VCOLS:(j + 1) * VCOLS, :], v_aug[:, buf2, kt, :],
                                   probs[:, kt % 2, j, :], start=kt == 0, stop=kt == TILES - 1,
                                   skip_group_check=True)
                mm.then_inc(pv_done, 1)

            def ring_ops(ops, k, i, l):
                h, buf = head(i, l)
                for kind, ahead, unit in ops:
                    if kind == "cut":
                        continue
                    if kind == "max" and unit == 0:
                        pe.wait_ge(stack_in[(buf + ahead) % STACKS], use(i, l, ahead) * LOADS * DMA)
                    if kind == "neg":
                        pe.wait_ge(neg_cut, h + ahead + 1)
                    if kind == "ctx":
                        pe.wait_ge(pv_copied, h + ahead + 1)
                    work = list_products(kind, unit, k, (buf + ahead) % STACKS)
                    for mm in work:
                        yield
                    k = k + 1

            def list_products(kind, unit, k, buf):
                left = {"max": 2, "neg": 1, "ctx": 1}[kind]
                for mm in ring_op(kind, unit, k, buf):
                    left -= 1
                    if not left:
                        mm.then_inc(ring_filled, 1)
                    yield mm

            def period(i, l, first=False, heads_after=2):
                h, buf = head(i, l)
                k = ring_base(h)
                pe.wait_ge(neg_in[buf], use(i, l) * PARTS * DMA)
                for kt, ops in enumerate(period_ops(first, heads_after)):
                    work = ring_ops(ops, k, i, l)
                    k = k + ring_len(ops)
                    for j in range(BLOCKS):
                        n = kt * BLOCKS + j
                        bank, back = score_bank(n)
                        pe.wait_ge(exps_done, SCORE_CREDIT + h * UNITS + n - back + 1)
                        pe.matmul(score_ps[bank][:, :], k_stack[0:ROWS_M, buf, kt * P:(kt + 1) * P],
                                  q_stack[0:ROWS_M, buf, j * TOK:(j + 1) * TOK],
                                  start=True, stop=True).then_inc(scores_ready, 1)
                        next(work, None)
                    for _ in work:
                        pass
                    if kt == 0:
                        if not first:
                            pv(h - 1, TILES - 1, (buf + 1) % 2)
                    else:
                        if kt == 1:
                            pe.wait_ge(v_aug_ready, h + 1)
                            if not first:
                                pe.wait_ge(pv_copied, h)
                        pv(h, kt - 1, buf % 2)

            pe.wait_ge(ones_set, 2)
            pe.wait_ge(raw_ready, 4 * A_GROUPS)
            pe.wait_ge(v_stored, 2 * A_GROUPS)
            for _ in ring_ops(OPENING, 0, -1, STACKS - 1):
                pass
            period(-1, STACKS - 1, first=True)
            with pe.Fori(0, LOOPS) as i:
                for l in range(STACKS):
                    period(i, l)
            for l in range(STACKS - 1):
                period(LOOPS, l, heads_after=STACKS - 2 - l)
            pv(ALL_HEADS - 1, TILES - 1, (ALL_HEADS - 1) % 2)
            for _ in ring_ops([("ctx", 0, 0)], RING_TOTAL - 1, LOOPS, STACKS - 2):
                pass

            def turn(n):
                pe.wait_ge(y_ready, n + 1)
                after(pe, y_ch_ready, n)
                for c in range(CHUNKS):
                    for q in range(TPB):
                        mm = pe.transpose(score_ps[c][:, q * P:(q + 1) * P],
                                          y_blk[:, n % 3, q, c * P:(c + 1) * P], id32[:, :])
                mm.then_inc(y_turned, 1)

            def value(n):
                pe.wait_ge(key_ready, n + 1)
                after(pe, gated_ready, n)
                for q in range(TPB):
                    for c in range(CHUNKS):
                        mm = pe.matmul(ring_ps[1][:, q * DIM:(q + 1) * DIM],
                                       key_act[:, n % 2, c, q * P:(q + 1) * P], w_rkv_s[:, 2, c, :],
                                       start=c == 0, stop=c == CHUNKS - 1, skip_group_check=True)
                mm.then_inc(kv_ready, 1)

            pe.wait_ge(c_in, 2 * DMA)
            pe.wait_ge(ring_freed, RING_CREDIT + RING_TOTAL)
            turn(0)
            for n in range(A_GROUPS):
                if n + 1 < A_GROUPS:
                    turn(n + 1)
                pe.wait_ge(mixed_ready, n + 1)
                after(pe, gate_ready, n)
                for q in range(TPB):
                    for c in range(CHUNKS):
                        mm = pe.matmul(ring_ps[0][:, q * DIM:(q + 1) * DIM], mixed[:, 0, c, q * P:(q + 1) * P],
                                       w_rkv_s[:, 0, c, :], start=c == 0, stop=c == CHUNKS - 1,
                                       skip_group_check=True)
                mm.then_inc(r_ready, 1)
                after(pe, relu_ready, n)
                for m, o in enumerate((score_ps[2], pv_ps)):
                    for c in range(CHUNKS):
                        mm = pe.matmul(o[:, :], w_rkv_s[:, 1, c, m * P:(m + 1) * P], mixed[:, 1, c, :],
                                       start=c == 0, stop=c == CHUNKS - 1)
                mm.then_inc(k_ready, 1)
                if n:
                    value(n - 1)
            value(A_GROUPS - 1)

        @block.scalar
        def _(act):
            n_in = 0
            for dst, src in ((w_qk_s, w_qk.rearrange("(c p) m -> p c m", p=P)),
                             (w_v_s, w_v.rearrange("(c p) n -> p c n", p=P)),
                             (b_qk_s, b_qk), (b_v_s, b_v.partition_broadcast(P)),
                             (cos_s, cos_t), (sin_s, sin_t), (id32[:, :], ident), (id16[:, :], ident_h)):
                act.dma_start(dst, src).then_inc(weights_in, DMA)
                n_in += 1
            assert n_in == 8
            act.wait_ge(weights_in, 8 * DMA)

            def take(n, i):
                act.wait_ge(qk_ready, 4 * n + i + 1)
                if i == 0:
                    after(act, rot_ready, n - 1)
                act.activation(raw[:, n % 2, i, :], ring_ps[i // 2][:, (i % 2) * TOK:(i % 2 + 1) * TOK],
                               ACT.Identity, bias=b_qk_s[:, i:i + 1]).then_inc(raw_ready, 1)

            def cut_high(n):
                act.wait_ge(rot_ready, n + 1)
                after(act, parts_out[n % 2], n // 2 * DMA)
                act.activation(cuts[:, n % 2, :, 0], rot[:, n % 2], ACT.Copy).then_inc(high_ready, 1)

            def cut_mid(n):
                act.wait_ge(rest_ready, n + 1)
                act.activation(cuts[:, n % 2, :, 1], rest[:, n % 2], ACT.Copy).then_inc(mid_ready, 1)

            for n in range(A_GROUPS + 2):
                if n >= 2:
                    cut_mid(n - 2)
                for i in range(4):
                    if i == 2 and 1 <= n <= A_GROUPS:
                        cut_high(n - 1)
                    if n < A_GROUPS:
                        take(n, i)

            act.sem_inc(exps_done, SCORE_CREDIT)

            def period(i, l, first=False):
                h, _ = head(i, l)
                for kt in range(TILES):
                    if kt == 1 and not first:
                        copy_pv(h)
                    act.wait_ge(pv_done, h * TILES + kt + 1)
                    for j in range(BLOCKS):
                        n = kt * BLOCKS + j
                        act.wait_ge(scores_ready, h * UNITS + n + 1)
                        act.activation(probs[:, kt % 2, j, :], score_ps[score_bank(n)[0]][:, :], ACT.Exp,
                                       scale=SCALE).then_inc(exps_done, 1)

            def copy_pv(h):
                act.wait_ge(pv_done, PV_CREDIT + h * TILES)
                if not isinstance(h, int) or h > 1:
                    act.wait_ge(recip_ready, h)
                act.copy(ctx_turn, pv_ps[:, :]).then_inc(pv_copied, 1)

            period(-1, STACKS - 1, first=True)
            with act.Fori(0, LOOPS) as i:
                for l in range(STACKS):
                    period(i, l)
            for l in range(STACKS - 1):
                period(LOOPS, l)
            copy_pv(ALL_HEADS)

            def std_of(lo, hi, signal):
                act.wait_ge(moments_ready, signal)
                act.activation(std[:, lo:hi], moments[:, lo:hi, 1], ACT.Sqrt, bias=eps_s).then_inc(std_ready, 1)

            def take_turned(n):
                act.wait_ge(y_turned, n + 1)
                after(act, mixed_ready, n)
                for c in range(CHUNKS):
                    ins = act.copy(y_ch[:, n % 2, c, 1:TOK + 1], score_ps[c][:, :])
                ins.then_inc(y_ch_ready, 1)
                act.wait_ge(edge_ready, n + 1)
                act.wait_ge(y_ch_ready, n + 1)
                for w in range(2):
                    for c in range(CHUNKS):
                        ins = act.mul(prev_part[:, w, c, :], y_ch[:, n % 2, c, 0:TOK], mu_c[:, w, c:c + 1])
                ins.then_inc(prev_ready, 1)

            act.wait_ge(c_small, 1)
            std_of(0, BATCH * TILES, BATCH * TILES)
            take_turned(0)
            for n in range(A_GROUPS):
                if n + 1 < A_GROUPS:
                    take_turned(n + 1)
                act.wait_ge(r_ready, n + 1)
                after(act, gated_ready, n - 1)
                act.activation(gate[:, n % 2].rearrange("p t d -> p (t d)"), ring_ps[0][:, :], ACT.Sigmoid)\
                    .then_inc(gate_ready, 1)
                act.wait_ge(k_ready, n + 1)
                after(act, key_ready, n)
                for c, o in enumerate((score_ps[2], pv_ps)):
                    ins = act.activation(relu[:, c, :], o[:, :], ACT.Relu)
                ins.then_inc(relu_ready, 1)
                if n == EARLY_OUT:
                    std_of(0, EARLY_OUT * TPB, (BATCH * BLOCKS + EARLY_OUT) * TPB)
            std_of(EARLY_OUT * TPB, BATCH * TILES, 2 * BATCH * TILES)

        @block.gpsimd
        def _(pool):
            pool.memset(k_stack[ROWS:ROWS_M, :, :], 1.0).then_inc(ones_set, 1)
            pool.wait_ge(ones_set, 1)
            pool.memset(v_aug[:, :, :, HEAD_DIM + 1:VCOLS], 0.0)
            pool.memset(v_aug[:, :, :, HEAD_DIM:HEAD_DIM + 1], 1.0).then_inc(ones_set, 1)
            pool.wait_ge(weights_in, 8 * DMA)
            for n in range(A_GROUPS + 1):
                if n < A_GROUPS:
                    t = n % BLOCKS
                    sin_b = sin_s[:, t * TOK:(t + 1) * TOK].unsqueeze(1).broadcast_to([P, 2, TOK])
                    pool.wait_ge(raw_ready, 4 * n + 4)
                    after(pool, rot_ready, n)
                    pool.tensor_tensor(o_sin, raw[:, n % 2, 2:4, :], sin_b, ALU.mult).then_inc(pool_product, 1)
                if n:
                    pool.wait_ge(high_ready, n)
                    after(pool, low_ready, n - 2)
                    pool.tensor_tensor(rest[:, (n - 1) % 2], rot[:, (n - 1) % 2], cuts[:, (n - 1) % 2, :, 0],
                                       ALU.subtract).then_inc(rest_ready, 1)

            def lay_v(h, buf2, waits):
                if waits:
                    pool.wait_ge(pv_done, PV_CREDIT + (h - 1) * TILES)
                pool.tensor_copy(v_aug[:, buf2, :, 0:HEAD_DIM], v_all[:, h]).then_inc(v_aug_ready, 1)

            def add_context(h):
                pool.wait_ge(ring_freed, RING_CREDIT + ctx_read(h))
                z = z_heads[:, :, h, :]
                pool.tensor_tensor(z, z, ctx_all[:, h], ALU.add).then_inc(z_ready, 1)

            pool.wait_ge(v_stored, 2 * A_GROUPS)
            lay_v(0, 0, False)
            lay_v(1, 1, False)
            pool.wait_ge(x_tok_in, BATCH * DMA)
            z_heads = z_all.rearrange("p t b (h d) -> p t (b h) d", d=HEAD_DIM)
            with pool.Fori(0, ALL_HEADS // 2 - 1) as i:
                for l in range(2):
                    lay_v(2 * i + l + 2, l, True)
                    add_context(2 * i + l)
            for h in (ALL_HEADS - 2, ALL_HEADS - 1):
                add_context(h)

        @block.vector
        def _(dve):
            def rotate(n):
                t = n % BLOCKS
                cos_b, sin_b = (a[:, t * TOK:(t + 1) * TOK].unsqueeze(1).broadcast_to([P, 2, TOK])
                                for a in (cos_s, sin_s))
                even, odd = raw[:, n % 2, 0:2, :], raw[:, n % 2, 2:4, :]
                dve.wait_ge(raw_ready, 4 * n + 4)
                dve.tensor_tensor(e_cos, even, cos_b, ALU.mult)
                dve.tensor_tensor(o_cos, odd, cos_b, ALU.mult)
                dve.tensor_tensor(e_sin, even, sin_b, ALU.mult).then_inc(products, 1)
                dve.wait_ge(products, n + 1)
                dve.wait_ge(pool_product, n + 1)
                after(dve, rest_ready, n - 1)
                after(dve, high_ready, n - 1)
                dve.tensor_tensor(rot[:, n % 2, 0], e_cos, o_sin, ALU.subtract)
                dve.tensor_tensor(rot[:, n % 2, 1], o_cos, e_sin, ALU.add).then_inc(rot_ready, 1)

            def take_v(n):
                for half in range(2):
                    dve.wait_ge(v_ready, 2 * n + half + 1)
                    for k in range(2):
                        tile = TPB * (n % BLOCKS) + 2 * half + k
                        heads = slice(n // BLOCKS * HEADS, (n // BLOCKS + 1) * HEADS)
                        ins = dve.tensor_tensor(
                            v_all[:, heads, tile, :],
                            score_ps[half][:, k * DIM:(k + 1) * DIM].rearrange("p (h d) -> p h d", d=HEAD_DIM),
                            b_v_s.rearrange("p (h d) -> p h d", d=HEAD_DIM), ALU.add)
                    ins.then_inc(v_stored, 1)

            def cut_low(n):
                dve.wait_ge(mid_ready, n + 1)
                dve.tensor_tensor(cuts[:, n % 2, :, 2], rest[:, n % 2], cuts[:, n % 2, :, 1], ALU.subtract)\
                    .then_inc(low_ready, 1)

            dve.wait_ge(weights_in, 8 * DMA)
            for n in range(A_GROUPS + 2):
                if n >= 2:
                    cut_low(n - 2)
                if 1 <= n <= A_GROUPS:
                    take_v(n - 1)
                if n < A_GROUPS:
                    rotate(n)

            dve.sem_inc(recip_ready, 1)
            dve.sem_inc(ring_freed, RING_CREDIT)

            slot_of = [0]

            def ring_reads(ops, k, i, l):
                h, buf = head(i, l)
                for kind, ahead, unit in ops:
                    if kind == "cut":
                        dve.wait_ge(ring_freed, RING_CREDIT + k)
                        cut_maxima(h + ahead)
                        continue
                    slot = ring_ps[slot_of[0]]
                    slot_of[0] ^= 1
                    dve.wait_ge(ring_filled, k + 1)
                    if kind == "max":
                        dve.reduce_max(tile_max[:, unit // 2, unit % 2:unit % 2 + 1], slot[:, :], AX.X)\
                            .then_inc(ring_freed, 1)
                    elif kind == "neg":
                        if ahead:
                            dve.wait_ge(neg_in[buf], use(i, l) * PARTS * DMA)
                        dve.tensor_copy(neg_rows[0:PARTS * TILES, :], slot[0:PARTS * TILES, 0:P])\
                            .then_inc(ring_freed, 1)
                    else:
                        dve.wait_ge(ring_freed, RING_CREDIT + k)
                        turned = slot[:, 0:TOK].rearrange("p (c j v) -> p c j v", c=TPB, j=BLOCKS)
                        dve.reciprocal(recip, turned[:, :, :, HEAD_DIM]).then_inc(recip_ready, 1)
                        dve.wait_ge(recip_ready, h + ahead + 2)
                        o = ctx_all[:, h + ahead].rearrange("p (j c) d -> p c j d", c=TPB)
                        dve.tensor_tensor(o, turned[:, :, :, 0:HEAD_DIM],
                                          recip.unsqueeze(3).broadcast_to([P, TPB, BLOCKS, HEAD_DIM]), ALU.mult)\
                            .then_inc(ring_freed, 1)
                    k = k + 1

            def cut_maxima(h):
                dve.tensor_reduce(neg_max, tile_max, AX.X, ALU.max, negate=True).then_inc(neg_step, 1)
                dve.wait_ge(neg_step, h * 4 + 1)
                dve.tensor_copy(neg_cuts[:, 0, :], neg_max).then_inc(neg_step, 1)
                dve.wait_ge(neg_step, h * 4 + 2)
                dve.tensor_tensor(neg_rest, neg_max, neg_cuts[:, 0, :], ALU.subtract).then_inc(neg_step, 1)
                dve.wait_ge(neg_step, h * 4 + 3)
                dve.tensor_copy(neg_cuts[:, 1, :], neg_rest).then_inc(neg_step, 1)
                dve.wait_ge(neg_step, h * 4 + 4)
                dve.tensor_tensor(neg_cuts[:, 2, :], neg_rest, neg_cuts[:, 1, :], ALU.subtract)\
                    .then_inc(neg_cut, 1)

            def period(i, l, first=False, heads_after=2):
                h, _ = head(i, l)
                k = ring_base(h)
                for ops in period_ops(first, heads_after):
                    ring_reads(ops, k, i, l)
                    k = k + ring_len(ops)

            dve.wait_ge(low_ready, A_GROUPS)
            ring_reads(OPENING, 0, -1, STACKS - 1)
            period(-1, STACKS - 1, first=True)
            with dve.Fori(0, LOOPS) as i:
                for l in range(STACKS):
                    period(i, l)
            for l in range(STACKS - 1):
                period(LOOPS, l, heads_after=STACKS - 2 - l)
            ring_reads([("ctx", 0, 0)], RING_TOTAL - 1, LOOPS, STACKS - 2)

            def tile_stats(tile, count):
                dve.bn_stats(stats[:, tile, :], z_tile(tile)).then_inc(stat_step, 1)
                dve.wait_ge(stat_step, count)
                dve.bn_aggr(moments[:, tile, :], stats[:, tile, :]).then_inc(moments_ready, 1)

            def invert(lo, hi, signal):
                dve.wait_ge(std_ready, signal)
                dve.reciprocal(rstd[:, lo:hi], std[:, lo:hi]).then_inc(rstd_ready, 1)
                dve.wait_ge(rstd_ready, signal)

            def normalise(n):
                after(dve, y_turned, n - 1)
                for q in range(TPB):
                    tile = n * TPB + q
                    ins = dve.tensor_scalar(y_blk[:, n % 3, q, :], z_tile(tile), moments[:, tile, 0:1],
                                            rstd[:, tile:tile + 1], ALU.subtract, ALU.mult)
                ins.then_inc(y_ready, 1)

            def mix(n):
                if n % BLOCKS == 0:
                    after(dve, prev_ready, n - 1)
                    dve.memset(y_ch[:, n % 2, :, 0:1], 0.0).then_inc(edge_ready, 1)
                else:
                    dve.wait_ge(y_ch_ready, n)
                    dve.tensor_copy(y_ch[:, n % 2, :, 0:1], y_ch[:, (n + 1) % 2, :, TOK:TOK + 1])\
                        .then_inc(edge_ready, 1)
                dve.wait_ge(prev_ready, n + 1)
                after(dve, k_ready, n)
                for w in range(2):
                    for c in range(CHUNKS):
                        ins = dve.scalar_tensor_tensor(mixed[:, w, c, :], y_ch[:, n % 2, c, 1:TOK + 1],
                                                       mu_s[:, w, c:c + 1], prev_part[:, w, c, :],
                                                       ALU.mult, ALU.add)
                ins.then_inc(mixed_ready, 1)

            def finish(n):
                dve.wait_ge(kv_ready, n + 1)
                dve.wait_ge(gate_ready, n + 1)
                dve.tensor_tensor(gated.rearrange("p t d -> p (t d)"), ring_ps[1][:, :],
                                  gate[:, n % 2].rearrange("p t d -> p (t d)"), ALU.mult).then_inc(gated_ready, 1)
                dve.wait_ge(gated_ready, n + 1)
                dve.tensor_tensor(z_block(n), gated, y_blk[:, n % 3], ALU.add)\
                    .then_inc(z2_ready, 1)
                dve.wait_ge(z2_ready, n + 1)
                for q in range(TPB):
                    tile_stats(n * TPB + q, BATCH * TILES + n * TPB + q + 1)

            def give(lo, hi):
                for tile in range(lo, hi):
                    dve.tensor_scalar(z_tile(tile), z_tile(tile), moments[:, tile, 0:1],
                                      rstd[:, tile:tile + 1], ALU.subtract, ALU.mult).then_inc(out_ready, 1)

            dve.wait_ge(ring_freed, RING_CREDIT + RING_TOTAL)
            dve.wait_ge(c_in, 2 * DMA)
            dve.memset(eps_s, EPS)
            dve.tensor_scalar(mu_c, mu_s, -1.0, 1.0, ALU.mult, ALU.add).then_inc(c_small, 1)
            dve.wait_ge(z_ready, HEADS)
            for tile in range(BATCH * TILES):
                if tile == TILES:
                    dve.wait_ge(z_ready, ALL_HEADS)
                tile_stats(tile, tile + 1)
            invert(0, BATCH * TILES, 1)
            normalise(0)
            mix(0)
            normalise(1)
            for n in range(A_GROUPS):
                if n + 1 < A_GROUPS:
                    mix(n + 1)
                dve.wait_ge(relu_ready, n + 1)
                after(dve, kv_ready, n - 1)
                dve.tensor_tensor(key_act[:, n % 2], relu, relu, ALU.mult).then_inc(key_ready, 1)
                if n:
                    finish(n - 1)
                if n + 2 < A_GROUPS:
                    normalise(n + 2)
                if n == EARLY_OUT + 1:
                    invert(0, EARLY_OUT * TPB, 2)
                    give(0, EARLY_OUT * TPB)
            finish(A_GROUPS - 1)
            invert(EARLY_OUT * TPB, BATCH * TILES, 3)
            give(EARLY_OUT * TPB, BATCH * TILES)


def rotary_tables():
    inv = np.power(np.float32(10000.0), np.float32(-2.0) * np.arange(PAIRS, dtype=np.float32) / np.float32(HEAD_DIM))
    ang = np.arange(SEQ, dtype=np.float32)[None, :] * inv.astype(np.float32)[:, None]
    return (np.tile(np.cos(ang).astype(np.float32), (HEADS, 1)), np.tile(np.sin(ang).astype(np.float32), (HEADS, 1)))


def kernel(**inputs):
    import concourse.bacc as bacc
    from concourse.bass_utils import run_bass_kernel_spmd
    import ml_dtypes

    x = np.asarray(inputs["L0_attn_hidden_states"]).reshape(BATCH * SEQ, DIM)
    wq, wk, wv = (np.asarray(inputs[f"L0_attn_W{n}"]) for n in "qkv")
    bq, bk, bv = (np.asarray(inputs[f"L0_attn_b{n}"]) for n in "qkv")
    even, odd = np.arange(0, DIM, 2), np.arange(1, DIM, 2)
    cos_t, sin_t = rotary_tables()
    arrays = {
        "x_tok": x,
        "x_ch": np.ascontiguousarray(x.T).reshape(CHUNKS, P, BATCH * SEQ),
        "w_qk": np.concatenate([wq[:, even], wk[:, even], wq[:, odd], wk[:, odd]], axis=1),
        "b_qk": np.stack([bq[even], bk[even], bq[odd], bk[odd]], axis=1),
        "w_v": wv,
        "b_v": bv,
        "w_rkv": np.stack([np.asarray(inputs[f"L0_ffn_W_{n}"]).T for n in "rkv"]),
        "mu": np.stack([np.asarray(inputs[f"L0_ffn_mu_{n}"]).reshape(CHUNKS, P) for n in "rk"]).transpose(2, 0, 1),
        "cos_t": cos_t,
        "sin_t": sin_t,
        "ident": np.eye(P, dtype=np.float32),
        "ident_h": np.eye(P, dtype=ml_dtypes.bfloat16),
    }
    arrays = {n: np.ascontiguousarray(a) for n, a in arrays.items()}
    nc = bacc.Bacc("TRN2", target_bir_lowering=False, num_devices=1)
    args = [nc.dram_tensor(n, a.shape, mybir.dt.from_np(a.dtype), kind="ExternalInput").ap()
            for n, a in arrays.items()]
    out = nc.dram_tensor("out", (BATCH * SEQ, DIM), F32, kind="ExternalOutput").ap()
    build(nc, *args, out)
    r = run_bass_kernel_spmd(nc, [arrays], core_ids=[0])
    return r.results[0]["out"].reshape(BATCH, SEQ, DIM)
```

```python
from contextlib import ExitStack

import numpy as np

import concourse.bass as bass
from concourse import mybir

F32 = mybir.dt.float32
BF16 = mybir.dt.bfloat16
ALU = mybir.AluOpType
ACT = mybir.ActivationFunctionType
AX = mybir.AxisListType

BATCH, SEQ, DIM = 2, 2048, 256
HEADS, HEAD_DIM = 16, 16
PAIRS = HEAD_DIM // 2
P = 128
CHUNKS = DIM // P
TOK = 512
BLOCKS = SEQ // TOK
TILES = SEQ // P
DVE_LOWS = 5
CUT_BUFS = 3
TPB = TOK // P
ALL_HEADS = BATCH * HEADS
PARTS = 3
Q_BANDS = [(0, 3), (1, 2), (2, 1)]
K_BANDS = [(0, 3), (0, 2), (0, 1)]
BANDS = sum(n for _, n in Q_BANDS)
ROWS = BANDS * HEAD_DIM
ROWS_M = ROWS + PARTS
VCOLS = 32
SCALE = float(HEAD_DIM) ** -0.5
EPS = 1e-5
DMA = 16

STACKS = 4
SLIP = 54
UNITS = TILES * BLOCKS
LOADS = len(Q_BANDS) + len(K_BANDS)
SCORE_CREDIT = 3
PV_CREDIT = 2
RING_CREDIT = 2
MAX_UNITS = 2 * TILES
RING_PER_HEAD = MAX_UNITS + 2
LEAD = 3
EARLY = 2 * LEAD
NEG_CYCLE = TILES - LEAD + 1
CTX_CYCLE = 2
TURN_CYCLES = (5, 7, 14)
R_CYCLE = 10
POOL_OUT = BATCH * BLOCKS - 2
EARLY_BLOCKS = len(TURN_CYCLES)
LOOPS = ALL_HEADS // STACKS - 1
REGION = 23 * 1024


def score_bank(n):
    if n < SLIP:
        return n % 3, 3
    if n == SLIP:
        return (n - 2) % 3, 2
    return (n - 1) % 3, 2 if n == SLIP + 2 else 3


def build(nc, x_tok, x_ch, w_qk, b_qk, w_v, b_v, w_rkv, mu, cos_t, sin_t, ident, ident_h, out):
    parts_d = nc.dram_tensor("qk_parts", (BATCH * P, 2, PARTS, 2, SEQ), BF16, kind="Internal").ap()

    with ExitStack() as ctx:
        def sb(name, shape, dt=F32):
            return ctx.enter_context(nc.sbuf_tensor(name, shape, dt))

        def pb(name, shape):
            return ctx.enter_context(nc.psum_tensor(name, shape, F32))

        def sem(name):
            return ctx.enter_context(nc.semaphore(name))

        v_all = sb("v_all", [P, ALL_HEADS, TILES, HEAD_DIM])
        ctx_all = sb("ctx_all", [P, ALL_HEADS, TILES, HEAD_DIM])
        id32 = sb("id32", [P, P])
        id16 = sb("id16", [P, P], BF16)
        q_stack = sb("q_stack", [P, STACKS, SEQ], BF16)
        k_stack = sb("k_stack", [P, STACKS, SEQ], BF16)
        v_aug = sb("v_aug", [P, 2, TILES, VCOLS])
        tile_max = sb("tile_max", [P, 2, TILES, 2])
        neg_max = sb("neg_max", [P, TILES])
        neg_rest = sb("neg_rest", [P, TILES])
        neg_cuts = sb("neg_cuts", [P, PARTS, TILES], BF16)
        zeros = sb("zeros", [P, TILES])
        eps_s = sb("eps_s", [P, TILES])
        minus_half = sb("minus_half", [P, TILES])
        neg_rows = sb("neg_rows", [P, P], BF16)
        recip = sb("recip", [P, TPB, BLOCKS])

        region = sb("region", [P, REGION])
        taken = [0]

        def cut(words, dt=F32):
            a = region[:, taken[0]:taken[0] + words]
            taken[0] += words
            return a if dt == F32 else a.bitcast(dt)

        w_qk_s = cut(CHUNKS * 4 * P).rearrange("p (c m) -> p c m", c=CHUNKS)
        w_v_s = cut(CHUNKS * DIM).rearrange("p (c n) -> p c n", c=CHUNKS)
        b_qk_s = cut(4)
        b_v_s = cut(DIM)
        cos_s = cut(SEQ)
        sin_s = cut(SEQ)
        x_blk = cut(2 * CHUNKS * TOK).rearrange("p (b c t) -> p b c t", b=2, c=CHUNKS)
        raw = cut(2 * 4 * TOK).rearrange("p (b i t) -> p b i t", b=2, i=4)
        o_sin, e_sin = (cut(2 * TOK).rearrange("p (s t) -> p s t", s=2) for _ in range(2))
        free = ctx_all[:, :, :, :].rearrange("p h t d -> p (h t d)").rearrange(
            "p (w b e s t) -> p w b e s t", w=2, b=2, e=2, s=2)
        rot, rest = free[:, 0], free[:, 1]
        cuts = cut(CUT_BUFS * PARTS * 2 * TOK, BF16).rearrange("p (b e a s t) -> p b e a s t", b=CUT_BUFS, e=2, a=PARTS, s=2)
        taken[0] = 0
        probs = cut(2 * BLOCKS * TOK).rearrange("p (g j t) -> p g j t", g=2, j=BLOCKS)
        ctx_turn = cut(TOK)
        w_rkv_s = cut(3 * CHUNKS * DIM).rearrange("p (w c n) -> p w c n", w=3, c=CHUNKS)
        mu_s = cut(2 * CHUNKS).rearrange("p (w c) -> p w c", w=2)
        mu_c = cut(2 * CHUNKS).rearrange("p (w c) -> p w c", w=2)
        stats = cut(BATCH * TILES * 6).rearrange("p (t s) -> p t s", s=6)
        moments = cut(BATCH * TILES * 2).rearrange("p (t s) -> p t s", s=2)
        rstd = cut(BATCH * TILES)
        rstd2 = cut(BATCH * TILES)
        y_ch = cut(2 * CHUNKS * (TOK + 4)).rearrange("p (b c t) -> p b c t", b=2, c=CHUNKS)
        prev_part = cut(2 * CHUNKS * TOK).rearrange("p (w c t) -> p w c t", w=2, c=CHUNKS)
        gated = cut(TPB * DIM).rearrange("p (t d) -> p t d", t=TPB)
        key_act = cut(2 * CHUNKS * TOK).rearrange("p (b c t) -> p b c t", b=2, c=CHUNKS)
        assert taken[0] <= REGION - BATCH * TILES * DIM
        taken[0] = REGION - BATCH * TILES * DIM
        z_all = cut(BATCH * TILES * DIM).rearrange("p (t b d) -> p t b d", b=BATCH, d=DIM)
        free = v_all[:, :, :, :].rearrange("p h t d -> p (h t d)")
        y_blk = free[:, 0:4 * TPB * DIM].rearrange("p (b t d) -> p b t d", b=4, t=TPB)
        gate = free[:, 4 * TPB * DIM:6 * TPB * DIM].rearrange("p (b t d) -> p b t d", b=2, t=TPB)
        relu = free[:, 6 * TPB * DIM:7 * TPB * DIM].rearrange("p (c t) -> p c t", c=CHUNKS)
        mixed = ctx_all[:, 0:HEADS].rearrange("p h t d -> p (h t d)").rearrange(
            "p (b w c t) -> p b w c t", b=2, w=2, c=CHUNKS)

        score_ps = [pb(f"score_ps{i}", [P, TOK]) for i in range(3)]
        ring_ps = [pb(f"ring_ps{i}", [P, 2 * TOK]) for i in range(2)]
        pv_ps = pb("pv_ps", [P, TOK])
        v_ps = (score_ps[0:2], (score_ps[2], pv_ps))

        w_qk_in = sem("w_qk_in")
        tables_in = sem("tables_in")
        w_v_in = sem("w_v_in")
        rest_in = sem("rest_in")
        x_in = [sem(f"x_in{i}") for i in range(2)]
        qk_ready = sem("qk_ready")
        v_ready = sem("v_ready")
        raw_ready = sem("raw_ready")
        v_stored = sem("v_stored")
        products = sem("products")
        pool_product = sem("pool_product")
        rot_ready = sem("rot_ready")
        high_ready = sem("high_ready")
        rest_ready = sem("rest_ready")
        mid_ready = sem("mid_ready")
        low_ready = sem("low_ready")
        parts_out = [sem(f"parts_out{i}") for i in range(CUT_BUFS)]
        stack_in = [sem(f"stack_in{i}") for i in range(STACKS)]
        ones_set = sem("ones_set")
        neg_in = [sem(f"neg_in{i}") for i in range(STACKS)]
        scores_ready = sem("scores_ready")
        exps_done = sem("exps_done")
        pv_done = sem("pv_done")
        pv_copied = sem("pv_copied")
        v_aug_ready = sem("v_aug_ready")
        ring_filled = sem("ring_filled")
        ring_freed = sem("ring_freed")
        neg_ready = sem("neg_ready")
        neg_step = sem("neg_step")
        neg_cut = sem("neg_cut")
        recip_ready = sem("recip_ready")
        x_tok_in = sem("x_tok_in")
        z_ready = sem("z_ready")
        c_in = sem("c_in")
        c_small = sem("c_small")
        stat_step = sem("stat_step")
        moments_ready = sem("moments_ready")
        eps_added = sem("eps_added")
        rstd_ready = sem("rstd_ready")
        rstd2_ready = sem("rstd2_ready")
        y_ready = sem("y_ready")
        y_turned = sem("y_turned")
        y_ch_ready = sem("y_ch_ready")
        edge_ready = sem("edge_ready")
        prev_ready = sem("prev_ready")
        mixed_ready = sem("mixed_ready")
        r_ready = sem("r_ready")
        k_ready = sem("k_ready")
        gate_ready = sem("gate_ready")
        relu_ready = sem("relu_ready")
        key_ready = sem("key_ready")
        kv_ready = sem("kv_ready")
        gated_ready = sem("gated_ready")
        z2_ready = sem("z2_ready")
        out_ready = sem("out_ready")
        last_ready = sem("last_ready")
        out_done = sem("out_done")

        block = ctx.enter_context(nc.Block())
        A_GROUPS = BATCH * BLOCKS

        def after(eng, signal, count):
            if count > 0:
                eng.wait_ge(signal, count)

        def z_tile(tile):
            return z_all[:, tile % TILES, tile // TILES, :]

        def z_block(n):
            t = n % BLOCKS * TPB
            return z_all[:, t:t + TPB, n // BLOCKS, :]

        def period_ops(first=False, heads_after=2):
            for kt in range(TILES):
                ops = []
                if kt == CTX_CYCLE and not first:
                    ops.append(("ctx", -1, 0))
                if kt == NEG_CYCLE and heads_after >= 1:
                    ops.append(("neg", 1, 0))
                for u in (2 * kt, 2 * kt + 1):
                    if u + EARLY < MAX_UNITS:
                        if heads_after >= 1:
                            ops.append(("max", 1, u + EARLY))
                            if u + EARLY == MAX_UNITS - 1:
                                ops.append(("cut", 1, 0))
                    elif heads_after >= 2:
                        ops.append(("max", 2, u + EARLY - MAX_UNITS))
                yield ops

        OPENING = [("max", 0, u) for u in range(MAX_UNITS)] + [("cut", 0, 0)]
        OPENING += [("max", 1, 0), ("max", 1, 1), ("neg", 0, 0)] + [("max", 1, u) for u in range(2, EARLY)]

        def ring_len(ops):
            return sum(kind != "cut" for kind, _, _ in ops)

        def ring_base(h):
            if isinstance(h, int) and h == 0:
                return ring_len(OPENING)
            if isinstance(h, int) and h == ALL_HEADS - 1:
                return ring_base(h - 1) + RING_PER_HEAD - EARLY
            return ring_len(OPENING) + h * RING_PER_HEAD - 1

        def ctx_read(h):
            if isinstance(h, int) and h >= ALL_HEADS - 2:
                return RING_TOTAL - (ALL_HEADS - 1 - h)
            return ring_base(h + 1) + 2 * CTX_CYCLE + 1

        def neg_read(h):
            known = isinstance(h, int)
            at = [op for ops in period_ops(known and h == 0, min(2, ALL_HEADS - 1 - h) if known else 2)
                  for op in ops]
            return ring_base(h) + ring_len(at[:at.index(("neg", 1, 0)) + 1])

        RING_TOTAL = ring_base(ALL_HEADS - 1) + 2
        turn_ps = ring_ps[ring_base(ALL_HEADS - 1) % 2]
        r_ps = ring_ps[(ring_base(ALL_HEADS - 1) + 1) % 2]
        value_ps = score_ps[0:2]
        key_ps = (score_ps[2], pv_ps)

        def head(i, l):
            return i * STACKS + 1 + l, (1 + l) % STACKS

        def use(i, l, ahead=0):
            return i + (1 + l + ahead) // STACKS + 1

        @block.sync
        def _(sp):
            def load_x(n):
                after(sp, v_ready, 2 * (n - 1))
                sp.dma_start(x_blk[:, n % 2], x_ch[:, :, n * TOK:(n + 1) * TOK].rearrange("c p t -> p c t"))\
                    .then_inc(x_in[n % 2], DMA)

            def store_parts(n):
                b, t = n // BLOCKS, n % BLOCKS
                sp.wait_ge(low_ready, n + 1)
                sp.dma_start(parts_d[b * P:(b + 1) * P, :, :, :, t * TOK:(t + 1) * TOK].rearrange(
                    "r e a s t -> r (e a s) t"), cuts[:, n % CUT_BUFS].rearrange("p e a s t -> p (e a s) t"))\
                    .then_inc(parts_out[n % CUT_BUFS], DMA)

            def load_stacks(h, buf):
                band = 0
                for a, reps in Q_BANDS:
                    src = parts_d[bass.ds(h * PAIRS, PAIRS), :, a, 0, :].rearrange("i e t -> (i e) t")
                    sp.dma_start(q_stack[band * HEAD_DIM:(band + reps) * HEAD_DIM, buf, :],
                                 src.unsqueeze(0).broadcast_to([reps, HEAD_DIM, SEQ])).then_inc(stack_in[buf], DMA)
                    band += reps
                band = 0
                for a, reps in K_BANDS:
                    src = parts_d[bass.ds(h * PAIRS, PAIRS), :, a:a + reps, 1, :]
                    sp.dma_start(k_stack[band * HEAD_DIM:(band + reps) * HEAD_DIM, buf, :],
                                 src.rearrange("i e a t -> a (i e) t")).then_inc(stack_in[buf], DMA)
                    band += reps

            def load_neg(reads, buf):
                sp.wait_ge(ring_freed, RING_CREDIT + reads)
                for a in range(PARTS):
                    sp.dma_start(q_stack[ROWS + a:ROWS + a + 1, buf, :],
                                 neg_rows[a * TILES:(a + 1) * TILES, :]).then_inc(neg_in[buf], DMA)

            load_x(0)
            load_x(1)
            load_x(2)
            load_x(3)
            for n in range(A_GROUPS):
                if n + 4 < A_GROUPS:
                    load_x(n + 4)
                if n == BLOCKS:
                    for i in range(CUT_BUFS):
                        sp.wait_ge(parts_out[i], DMA * len(range(i, BLOCKS, CUT_BUFS)))
                if n >= BLOCKS:
                    load_stacks(n - BLOCKS, n - BLOCKS)
                store_parts(n)
            load_neg(ring_len(OPENING[:OPENING.index(("neg", 0, 0)) + 1]), 0)
            sp.wait_ge(v_stored, 2 * A_GROUPS)
            for i in range(CUT_BUFS):
                sp.wait_ge(parts_out[i], DMA * len(range(i, A_GROUPS, CUT_BUFS)))
            for b in range(BATCH):
                sp.dma_start(z_all[:, :, b, :], x_tok[b * SEQ:(b + 1) * SEQ, :].rearrange("(t p) d -> p t d", p=P))\
                    .then_inc(x_tok_in, DMA)
            sp.dma_start(w_rkv_s, w_rkv.rearrange("w (c p) n -> p w c n", p=P)).then_inc(c_in, DMA)
            sp.dma_start(mu_s, mu).then_inc(c_in, DMA)

            def period(i, l, refill=True, last=False):
                h, buf = head(i, l)
                if not last:
                    load_neg(neg_read(h), (buf + 1) % STACKS)
                if refill:
                    sp.wait_ge(scores_ready, (h + 1) * UNITS)
                    load_stacks(h + STACKS, buf)

            period(-1, STACKS - 1)
            with sp.Fori(0, LOOPS - 1) as i:
                for l in range(STACKS):
                    period(i, l)
            for n in range((LOOPS - 1) * STACKS, ALL_HEADS - 1):
                period(n // STACKS, n % STACKS, n + 1 + STACKS < ALL_HEADS, n + 1 == ALL_HEADS - 1)

            out_t = out.rearrange("(t p) d -> p t d", p=P)
            for g in range(A_GROUPS):
                if g < POOL_OUT:
                    sp.wait_ge(out_ready, g + 1)
                else:
                    sp.wait_ge(last_ready, g + 1 - POOL_OUT)
                sp.dma_start(out_t[:, g * TPB:(g + 1) * TPB, :], z_block(g))\
                    .then_inc(out_done, DMA)
            sp.wait_ge(out_done, DMA * A_GROUPS)

        @block.tensor
        def _(pe):
            pe.sem_inc(pv_done, PV_CREDIT)
            pe.wait_ge(w_qk_in, 2 * DMA)
            for n in range(A_GROUPS):
                par = n % 2
                pe.wait_ge(x_in[par], (n // 2 + 1) * DMA)
                for i in range(4):
                    after(pe, raw_ready, 4 * (n - 1) + i + 1)
                    o = ring_ps[i // 2][:, (i % 2) * TOK:(i % 2 + 1) * TOK]
                    for c in range(CHUNKS):
                        mm = pe.matmul(o, w_qk_s[:, c, i * P:(i + 1) * P], x_blk[:, par, c, :],
                                       start=c == 0, stop=c == CHUNKS - 1)
                    mm.then_inc(qk_ready, 1)
                if n == 0:
                    pe.wait_ge(w_v_in, 2 * DMA)
                for half in range(2):
                    after(pe, v_stored, 2 * (n - 2) + half + 1)
                    for k in range(2):
                        lo = (2 * half + k) * P
                        for c in range(CHUNKS):
                            mm = pe.matmul(v_ps[n % 2][half][:, k * DIM:(k + 1) * DIM],
                                           x_blk[:, par, c, lo:lo + P], w_v_s[:, c, :],
                                           start=c == 0, stop=c == CHUNKS - 1, skip_group_check=True)
                    mm.then_inc(v_ready, 1)

            def ring_op(kind, unit, k, buf):
                slot = ring_ps[slot_of[0]]
                slot_of[0] ^= 1
                pe.wait_ge(ring_freed, k + 1)
                if kind == "max":
                    qt, half = unit // 2, unit % 2
                    for c in range(2):
                        lo = (2 * half + c) * TOK
                        yield pe.matmul(slot[:, c * TOK:(c + 1) * TOK], q_stack[0:ROWS, buf, qt * P:(qt + 1) * P],
                                        k_stack[0:ROWS, buf, lo:lo + TOK], start=True, stop=True)
                elif kind == "neg":
                    yield neg_product(slot)
                else:
                    for c in range(TPB):
                        mm = pe.transpose(slot[:, c * P:(c + 1) * P], ctx_turn[:, c * P:(c + 1) * P], id32[:, :])
                    yield mm

            slot_of = [0]

            def neg_product(slot):
                return pe.matmul(slot[0:PARTS * TILES, 0:P], neg_cuts[:, :, :].rearrange("p a t -> p (a t)"), id16[:, :],
                                 start=True, stop=True)

            def pv(h, kt, buf2):
                for j in range(BLOCKS):
                    pe.wait_ge(exps_done, SCORE_CREDIT + h * UNITS + kt * BLOCKS + j + 1)
                    mm = pe.matmul(pv_ps[j * VCOLS:(j + 1) * VCOLS, :], v_aug[:, buf2, kt, :],
                                   probs[:, kt % 2, j, :], start=kt == 0, stop=kt == TILES - 1,
                                   skip_group_check=True)
                mm.then_inc(pv_done, 1)

            def ring_ops(ops, k, i, l):
                h, buf = head(i, l)
                for kind, ahead, unit in ops:
                    if kind == "cut":
                        continue
                    if kind == "max" and unit == 0:
                        pe.wait_ge(stack_in[(buf + ahead) % STACKS], use(i, l, ahead) * LOADS * DMA)
                    if kind == "neg":
                        pe.wait_ge(neg_cut, h + ahead + 1)
                    if kind == "ctx":
                        pe.wait_ge(pv_copied, h + ahead + 1)
                    work = list_products(kind, unit, k, (buf + ahead) % STACKS)
                    for _ in work:
                        yield
                    k = k + 1

            def list_products(kind, unit, k, buf):
                left = {"max": 2, "neg": 1, "ctx": 1}[kind]
                for mm in ring_op(kind, unit, k, buf):
                    left -= 1
                    if not left:
                        mm.then_inc(ring_filled, 1)
                    yield mm

            def turn(n):
                pe.wait_ge(y_ready, n + 1)
                after(pe, y_ch_ready, n)
                for c in range(CHUNKS):
                    for q in range(TPB):
                        mm = pe.transpose(turn_ps[:, c * TOK + q * P:c * TOK + (q + 1) * P],
                                          y_blk[:, n % 4, q, c * P:(c + 1) * P], id32[:, :])
                        if (c, q) == (CHUNKS - 1, TPB - 1):
                            mm.then_inc(y_turned, 1)
                        yield

            def project_r(n):
                pe.wait_ge(mixed_ready, n + 1)
                after(pe, gate_ready, n)
                for q in range(TPB):
                    for c in range(CHUNKS):
                        mm = pe.matmul(r_ps[:, q * DIM:(q + 1) * DIM], mixed[:, n % 2, 0, c, q * P:(q + 1) * P],
                                       w_rkv_s[:, 0, c, :], start=c == 0, stop=c == CHUNKS - 1,
                                       skip_group_check=True)
                        if (q, c) == (TPB - 1, CHUNKS - 1):
                            mm.then_inc(r_ready, 1)
                        yield

            def beside(kt):
                if kt == TURN_CYCLES[0]:
                    pe.wait_ge(ring_freed, RING_CREDIT + RING_TOTAL - 1)
                    return turn(0)
                if kt in TURN_CYCLES:
                    return turn(TURN_CYCLES.index(kt))
                if kt == R_CYCLE:
                    return project_r(0)
                return None

            def period(i, l, first=False, heads_after=2):
                h, buf = head(i, l)
                k = ring_base(h)
                stage_c = iter(())
                pe.wait_ge(neg_in[buf], use(i, l) * PARTS * DMA)
                for kt, ops in enumerate(period_ops(first, heads_after)):
                    work = ring_ops(ops, k, i, l)
                    k = k + ring_len(ops)
                    for j in range(BLOCKS):
                        n = kt * BLOCKS + j
                        bank, back = score_bank(n)
                        pe.wait_ge(exps_done, SCORE_CREDIT + h * UNITS + n - back + 1)
                        pe.matmul(score_ps[bank][:, :], k_stack[0:ROWS_M, buf, kt * P:(kt + 1) * P],
                                  q_stack[0:ROWS_M, buf, j * TOK:(j + 1) * TOK],
                                  start=True, stop=True).then_inc(scores_ready, 1)
                        next(work, None)
                        if heads_after == 0:
                            if j == 0:
                                stage_c = beside(kt) or stage_c
                            if not R_CYCLE <= kt < TURN_CYCLES[-1] or j % 2:
                                next(stage_c, None)
                    for _ in work:
                        pass
                    if kt == 0:
                        if not first:
                            pv(h - 1, TILES - 1, (buf + 1) % 2)
                    else:
                        if kt == 1:
                            pe.wait_ge(v_aug_ready, h + 1)
                            if not first:
                                pe.wait_ge(pv_copied, h)
                        pv(h, kt - 1, buf % 2)
                for _ in stage_c:
                    pass

            pe.wait_ge(ones_set, 2)
            pe.wait_ge(rest_in, 4 * DMA)
            pe.wait_ge(raw_ready, 4 * A_GROUPS)
            for _ in ring_ops(OPENING, 0, -1, STACKS - 1):
                pass
            pe.wait_ge(v_stored, 2 * A_GROUPS)
            period(-1, STACKS - 1, first=True)
            with pe.Fori(0, LOOPS) as i:
                for l in range(STACKS):
                    period(i, l)
            for l in range(STACKS - 1):
                if l == STACKS - 2:
                    pe.wait_ge(c_in, 2 * DMA)
                period(LOOPS, l, heads_after=STACKS - 2 - l)
            pv(ALL_HEADS - 1, TILES - 1, (ALL_HEADS - 1) % 2)
            slot_of[0] ^= 1
            pe.wait_ge(y_ch_ready, EARLY_BLOCKS)
            for _ in ring_ops([("ctx", 0, 0)], RING_TOTAL - 1, LOOPS, STACKS - 2):
                pass

            def value(n):
                pe.wait_ge(key_ready, n + 1)
                after(pe, gated_ready, 2 * n)
                for q in range(TPB):
                    for c in range(CHUNKS):
                        mm = pe.matmul(value_ps[q // 2][:, q % 2 * DIM:(q % 2 + 1) * DIM],
                                       key_act[:, n % 2, c, q * P:(q + 1) * P], w_rkv_s[:, 2, c, :],
                                       start=c == 0, stop=c == CHUNKS - 1, skip_group_check=True)
                    if q % 2:
                        mm.then_inc(kv_ready, 1)

            def project_key(n):
                pe.wait_ge(mixed_ready, n + 1)
                after(pe, relu_ready, n)
                for m, o in enumerate(key_ps):
                    for c in range(CHUNKS):
                        mm = pe.matmul(o[:, :], w_rkv_s[:, 1, c, m * P:(m + 1) * P], mixed[:, n % 2, 1, c, :],
                                       start=c == 0, stop=c == CHUNKS - 1)
                mm.then_inc(k_ready, 1)

            project_key(0)
            pe.wait_ge(ring_freed, RING_CREDIT + RING_TOTAL)
            for n in range(1, A_GROUPS):
                if EARLY_BLOCKS <= n + 1 < A_GROUPS:
                    for _ in turn(n + 1):
                        pass
                if n + 1 < A_GROUPS:
                    for _ in project_r(n):
                        pass
                    value(n - 1)
                    project_key(n)
                else:
                    project_key(n)
                    value(n - 1)
                    for _ in project_r(n):
                        pass
            value(A_GROUPS - 1)

        @block.scalar
        def _(act):
            for dst, src, signal in (
                    (w_qk_s, w_qk.rearrange("(c p) m -> p c m", p=P), w_qk_in), (b_qk_s, b_qk, w_qk_in),
                    (cos_s[:, 0:TOK], cos_t[:, 0:TOK], tables_in), (sin_s[:, 0:TOK], sin_t[:, 0:TOK], tables_in),
                    (w_v_s, w_v.rearrange("(c p) n -> p c n", p=P), w_v_in), (b_v_s, b_v.partition_broadcast(P), w_v_in),
                    (cos_s[:, TOK:SEQ], cos_t[:, TOK:SEQ], rest_in), (sin_s[:, TOK:SEQ], sin_t[:, TOK:SEQ], rest_in),
                    (id32[:, :], ident, rest_in), (id16[:, :], ident_h, rest_in)):
                act.dma_start(dst, src).then_inc(signal, DMA)
            act.wait_ge(w_qk_in, 2 * DMA)

            def take(n, i):
                act.wait_ge(qk_ready, 4 * n + i + 1)
                if i == 0:
                    after(act, rot_ready, n - 1)
                act.activation(raw[:, n % 2, i, :], ring_ps[i // 2][:, (i % 2) * TOK:(i % 2 + 1) * TOK],
                               ACT.Identity, bias=b_qk_s[:, i:i + 1]).then_inc(raw_ready, 1)

            def cut_high(n):
                act.wait_ge(rot_ready, n + 1)
                after(act, parts_out[n % CUT_BUFS], n // CUT_BUFS * DMA)
                act.activation(cuts[:, n % CUT_BUFS, :, 0], rot[:, n % 2], ACT.Copy).then_inc(high_ready, 1)

            def cut_mid(n):
                act.wait_ge(rest_ready, n + 1)
                act.activation(cuts[:, n % CUT_BUFS, :, 1], rest[:, n % 2], ACT.Copy).then_inc(mid_ready, 1)

            for n in range(A_GROUPS + 2):
                for i in range(4):
                    if i == 2 and 1 <= n <= A_GROUPS:
                        cut_high(n - 1)
                    if n < A_GROUPS:
                        take(n, i)
                if n >= 2:
                    cut_mid(n - 2)

            act.sem_inc(exps_done, SCORE_CREDIT)

            def period(i, l, first=False):
                h, _ = head(i, l)
                for kt in range(TILES):
                    if kt == 1 and not first:
                        copy_pv(h)
                    act.wait_ge(pv_done, h * TILES + kt + 1)
                    for j in range(BLOCKS):
                        n = kt * BLOCKS + j
                        act.wait_ge(scores_ready, h * UNITS + n + 1)
                        act.activation(probs[:, kt % 2, j, :], score_ps[score_bank(n)[0]][:, :], ACT.Exp,
                                       scale=SCALE).then_inc(exps_done, 1)

            def copy_pv(h):
                act.wait_ge(pv_done, PV_CREDIT + h * TILES)
                if not isinstance(h, int) or h > 1:
                    act.wait_ge(recip_ready, h)
                act.copy(ctx_turn, pv_ps[:, :]).then_inc(pv_copied, 1)

            period(-1, STACKS - 1, first=True)
            with act.Fori(0, LOOPS) as i:
                for l in range(STACKS):
                    period(i, l)
            for l in range(STACKS - 1):
                period(LOOPS, l)
            copy_pv(ALL_HEADS)

            def take_turned(n):
                act.wait_ge(y_turned, n + 1)
                after(act, mixed_ready, n)
                for c in range(CHUNKS):
                    ins = act.copy(y_ch[:, n % 2, c, 1:TOK + 1], turn_ps[:, c * TOK:(c + 1) * TOK])
                ins.then_inc(y_ch_ready, 1)
                act.wait_ge(edge_ready, n + 1)
                act.wait_ge(y_ch_ready, n + 1)
                for w in range(2):
                    for c in range(CHUNKS):
                        ins = act.mul(prev_part[:, w, c, :], y_ch[:, n % 2, c, 0:TOK], mu_c[:, w, c:c + 1])
                ins.then_inc(prev_ready, 1)

            def sigmoid(n):
                act.wait_ge(r_ready, n + 1)
                after(act, gated_ready, 2 * (n - 1))
                act.activation(gate[:, n % 2].rearrange("p t d -> p (t d)"), r_ps[:, :], ACT.Sigmoid)\
                    .then_inc(gate_ready, 1)

            def take_key(n):
                act.wait_ge(k_ready, n + 1)
                after(act, key_ready, n)
                for c, o in enumerate(key_ps):
                    ins = act.activation(relu[:, c, :], o[:, :], ACT.Relu)
                ins.then_inc(relu_ready, 1)

            act.wait_ge(c_small, 1)
            for n in range(A_GROUPS):
                if EARLY_BLOCKS <= n + 1 < A_GROUPS:
                    take_turned(n + 1)
                if n + 1 < A_GROUPS:
                    sigmoid(n)
                    take_key(n)
                else:
                    take_key(n)
                    sigmoid(n)

        @block.gpsimd
        def _(pool):
            pool.memset(k_stack[ROWS:ROWS_M, :, :], 1.0).then_inc(ones_set, 1)
            pool.wait_ge(ones_set, 1)
            pool.memset(zeros[:, :], 0.0)
            pool.memset(eps_s[:, :], EPS)
            pool.memset(minus_half[:, :], -0.5)
            pool.memset(v_aug[:, :, :, HEAD_DIM + 1:VCOLS], 0.0)
            pool.memset(v_aug[:, :, :, HEAD_DIM:HEAD_DIM + 1], 1.0).then_inc(ones_set, 1)
            pool.wait_ge(ones_set, 2)

            def cut_low(n):
                pool.wait_ge(mid_ready, n + 1)
                pool.wait_ge(low_ready, n)
                pool.tensor_tensor(cuts[:, n % CUT_BUFS, :, 2], rest[:, n % 2], cuts[:, n % CUT_BUFS, :, 1],
                                   ALU.subtract).then_inc(low_ready, 1)

            def rotate(n):
                t = n % BLOCKS
                cos_b, sin_b = (a[:, t * TOK:(t + 1) * TOK].unsqueeze(1).broadcast_to([P, 2, TOK])
                                for a in (cos_s, sin_s))
                even, odd = raw[:, n % 2, 0:2, :], raw[:, n % 2, 2:4, :]
                pool.wait_ge(raw_ready, 4 * n + 4)
                pool.wait_ge(rot_ready, n)
                pool.wait_ge(rest_ready, n - 1)
                pool.wait_ge(high_ready, n - 1)
                pool.tensor_tensor(rot[:, n % 2, 0], even, cos_b, ALU.mult)
                pool.tensor_tensor(rot[:, n % 2, 1], odd, cos_b, ALU.mult)
                pool.tensor_tensor(o_sin, odd, sin_b, ALU.mult)
                pool.tensor_tensor(e_sin, even, sin_b, ALU.mult).then_inc(pool_product, 1)
                pool.wait_ge(pool_product, n + 1)
                pool.tensor_tensor(rot[:, n % 2, 0], rot[:, n % 2, 0], o_sin, ALU.subtract)
                pool.tensor_tensor(rot[:, n % 2, 1], rot[:, n % 2, 1], e_sin, ALU.add).then_inc(rot_ready, 1)

            pool.wait_ge(tables_in, 2 * DMA)
            for n in range(A_GROUPS + 1):
                if n == 1:
                    pool.wait_ge(rest_in, 4 * DMA)
                if n < A_GROUPS - 1:
                    t = n % BLOCKS
                    sin_b = sin_s[:, t * TOK:(t + 1) * TOK].unsqueeze(1).broadcast_to([P, 2, TOK])
                    pool.wait_ge(raw_ready, 4 * n + 4)
                    after(pool, rot_ready, n)
                    pool.tensor_tensor(o_sin, raw[:, n % 2, 2:4, :], sin_b, ALU.mult).then_inc(pool_product, 1)
                if n == A_GROUPS:
                    cut_low(n - 2)
                if n:
                    pool.wait_ge(high_ready, n)
                    after(pool, low_ready, n - 2)
                    pool.tensor_tensor(rest[:, (n - 1) % 2], rot[:, (n - 1) % 2], cuts[:, (n - 1) % CUT_BUFS, :, 0],
                                       ALU.subtract).then_inc(rest_ready, 1)
                if DVE_LOWS + 2 <= n < A_GROUPS:
                    cut_low(n - 2)
                if n == A_GROUPS - 1:
                    rotate(n)
            cut_low(A_GROUPS - 1)

            def lay_v(h, buf2, waits):
                if waits:
                    pool.wait_ge(pv_done, PV_CREDIT + (h - 1) * TILES)
                nothing = zeros[:, :].unsqueeze(2).broadcast_to([P, TILES, HEAD_DIM])
                pool.tensor_tensor(v_aug[:, buf2, :, 0:HEAD_DIM], v_all[:, h], nothing, ALU.add)\
                    .then_inc(v_aug_ready, 1)

            def cut_maxima(h):
                pool.wait_ge(neg_ready, h + 1)
                pool.tensor_tensor(neg_cuts[:, 0, :], neg_max[:, :], zeros[:, :], ALU.add).then_inc(neg_step, 1)
                pool.wait_ge(neg_step, h * 3 + 1)
                pool.tensor_tensor(neg_rest[:, :], neg_max[:, :], neg_cuts[:, 0, :], ALU.subtract).then_inc(neg_step, 1)
                pool.wait_ge(neg_step, h * 3 + 2)
                pool.tensor_tensor(neg_cuts[:, 1, :], neg_rest[:, :], zeros[:, :], ALU.add).then_inc(neg_step, 1)
                pool.wait_ge(neg_step, h * 3 + 3)
                pool.tensor_tensor(neg_cuts[:, 2, :], neg_rest[:, :], neg_cuts[:, 1, :], ALU.subtract)\
                    .then_inc(neg_cut, 1)

            def add_context(h):
                pool.wait_ge(ring_freed, RING_CREDIT + ctx_read(h))
                z = z_heads[:, :, h, :]
                pool.tensor_tensor(z, z, ctx_all[:, h], ALU.add).then_inc(z_ready, 1)

            pool.wait_ge(v_stored, 2 * A_GROUPS)
            lay_v(0, 0, False)
            lay_v(1, 1, False)
            cut_maxima(0)
            pool.wait_ge(x_tok_in, BATCH * DMA)
            z_heads = z_all.rearrange("p t b (h d) -> p t (b h) d", d=HEAD_DIM)
            cut_maxima(1)
            with pool.Fori(0, ALL_HEADS // 2 - 1) as i:
                for l in range(2):
                    lay_v(2 * i + l + 2, l, True)
                    add_context(2 * i + l)
                    cut_maxima(2 * i + l + 2)

            eps_count = [0]

            def inverse(dst, lo, hi, count, signal):
                pool.wait_ge(moments_ready, count)
                pool.tensor_tensor(dst[:, lo:hi], moments[:, lo:hi, 1], eps_s[:, 0:hi - lo], ALU.add).then_inc(eps_added, 1)
                eps_count[0] += 1
                pool.wait_ge(eps_added, eps_count[0])
                pool.tensor_tensor(dst[:, lo:hi], dst[:, lo:hi], minus_half[:, 0:hi - lo], ALU.pow).then_inc(signal, 1)

            for b in range(BATCH):
                add_context(ALL_HEADS - 2 + b)
                inverse(rstd, b * TILES, (b + 1) * TILES, (b + 1) * TILES, rstd_ready)

            for n in range(A_GROUPS):
                inverse(rstd2, n * TPB, (n + 1) * TPB, BATCH * TILES + (n + 1) * TPB, rstd2_ready)
                if n >= POOL_OUT:
                    continue
                pool.wait_ge(rstd2_ready, n + 1)
                for tile in range(n * TPB, (n + 1) * TPB):
                    ins = pool.tensor_scalar(z_tile(tile), z_tile(tile), moments[:, tile, 0:1],
                                             rstd2[:, tile:tile + 1], ALU.subtract, ALU.mult)
                ins.then_inc(out_ready, 1)

        @block.vector
        def _(dve):
            def rotate(n):
                t = n % BLOCKS
                cos_b, sin_b = (a[:, t * TOK:(t + 1) * TOK].unsqueeze(1).broadcast_to([P, 2, TOK])
                                for a in (cos_s, sin_s))
                even, odd = raw[:, n % 2, 0:2, :], raw[:, n % 2, 2:4, :]
                dve.wait_ge(raw_ready, 4 * n + 4)
                after(dve, rest_ready, n - 1)
                after(dve, high_ready, n - 1)
                dve.tensor_tensor(rot[:, n % 2, 0], even, cos_b, ALU.mult)
                dve.tensor_tensor(rot[:, n % 2, 1], odd, cos_b, ALU.mult)
                dve.tensor_tensor(e_sin, even, sin_b, ALU.mult).then_inc(products, 1)
                dve.wait_ge(products, n + 1)
                dve.wait_ge(pool_product, n + 1)
                dve.tensor_tensor(rot[:, n % 2, 0], rot[:, n % 2, 0], o_sin, ALU.subtract)
                dve.tensor_tensor(rot[:, n % 2, 1], rot[:, n % 2, 1], e_sin, ALU.add).then_inc(rot_ready, 1)

            def take_v(n):
                for half in range(2):
                    dve.wait_ge(v_ready, 2 * n + half + 1)
                    for k in range(2):
                        tile = TPB * (n % BLOCKS) + 2 * half + k
                        heads = slice(n // BLOCKS * HEADS, (n // BLOCKS + 1) * HEADS)
                        ins = dve.tensor_tensor(
                            v_all[:, heads, tile, :],
                            v_ps[n % 2][half][:, k * DIM:(k + 1) * DIM].rearrange("p (h d) -> p h d", d=HEAD_DIM),
                            b_v_s.rearrange("p (h d) -> p h d", d=HEAD_DIM), ALU.add)
                    ins.then_inc(v_stored, 1)

            def cut_low(n):
                dve.wait_ge(mid_ready, n + 1)
                dve.tensor_tensor(cuts[:, n % CUT_BUFS, :, 2], rest[:, n % 2], cuts[:, n % CUT_BUFS, :, 1], ALU.subtract)\
                    .then_inc(low_ready, 1)

            dve.wait_ge(tables_in, 2 * DMA)
            for n in range(A_GROUPS):
                if n == 1:
                    dve.wait_ge(w_v_in, 2 * DMA)
                    dve.wait_ge(rest_in, 4 * DMA)
                if n:
                    take_v(n - 1)
                if n < A_GROUPS - 1:
                    rotate(n)
                if 2 <= n < DVE_LOWS + 2:
                    cut_low(n - 2)
            take_v(A_GROUPS - 1)

            dve.sem_inc(recip_ready, 1)
            dve.sem_inc(ring_freed, RING_CREDIT)

            slot_of = [0]

            def ring_reads(ops, k, i, l):
                h, buf = head(i, l)
                for kind, ahead, unit in ops:
                    parity = (buf + ahead) % 2
                    if kind == "cut":
                        dve.wait_ge(ring_freed, RING_CREDIT + k)
                        dve.tensor_reduce(neg_max[:, :], tile_max[:, parity], AX.X, ALU.max, negate=True)\
                            .then_inc(neg_ready, 1)
                        continue
                    slot = ring_ps[slot_of[0]]
                    slot_of[0] ^= 1
                    dve.wait_ge(ring_filled, k + 1)
                    if kind == "max":
                        if unit == 0 and ahead == 2:
                            dve.wait_ge(neg_ready, h + 1)
                        dve.reduce_max(tile_max[:, parity, unit // 2, unit % 2:unit % 2 + 1], slot[:, :], AX.X)\
                            .then_inc(ring_freed, 1)
                    elif kind == "neg":
                        if ahead:
                            dve.wait_ge(neg_in[buf], use(i, l) * PARTS * DMA)
                        dve.tensor_copy(neg_rows[0:PARTS * TILES, :], slot[0:PARTS * TILES, 0:P])\
                            .then_inc(ring_freed, 1)
                    else:
                        dve.wait_ge(ring_freed, RING_CREDIT + k)
                        turned = slot[:, 0:TOK].rearrange("p (c j v) -> p c j v", c=TPB, j=BLOCKS)
                        dve.reciprocal(recip[:, :, :], turned[:, :, :, HEAD_DIM]).then_inc(recip_ready, 1)
                        dve.wait_ge(recip_ready, h + ahead + 2)
                        o = ctx_all[:, h + ahead].rearrange("p (j c) d -> p c j d", c=TPB)
                        dve.tensor_tensor(o, turned[:, :, :, 0:HEAD_DIM],
                                          recip[:, :, :].unsqueeze(3).broadcast_to([P, TPB, BLOCKS, HEAD_DIM]), ALU.mult)\
                            .then_inc(ring_freed, 1)
                    k = k + 1

            stat_count = [0]

            def tile_stats(tiles):
                base = stat_count[0]
                stat_count[0] += len(tiles)
                for n, tile in enumerate([*tiles, None]):
                    if tile is not None:
                        dve.bn_stats(stats[:, tile, :], z_tile(tile)).then_inc(stat_step, 1)
                    if n:
                        dve.wait_ge(stat_step, base + n)
                        dve.bn_aggr(moments[:, tiles[n - 1], :], stats[:, tiles[n - 1], :]).then_inc(moments_ready, 1)

            def normalise(n):
                after(dve, y_turned, n - 1)
                for q in range(TPB):
                    tile = n * TPB + q
                    ins = dve.tensor_scalar(y_blk[:, n % 4, q, :], z_tile(tile), moments[:, tile, 0:1],
                                            rstd[:, tile:tile + 1], ALU.subtract, ALU.mult)
                ins.then_inc(y_ready, 1)

            def edge(n):
                if n % BLOCKS == 0:
                    after(dve, prev_ready, n - 1)
                    dve.memset(y_ch[:, n % 2, :, 0:1], 0.0).then_inc(edge_ready, 1)
                else:
                    dve.wait_ge(y_ch_ready, n)
                    dve.tensor_copy(y_ch[:, n % 2, :, 0:1], y_ch[:, (n + 1) % 2, :, TOK:TOK + 1])\
                        .then_inc(edge_ready, 1)

            def take_turned(n):
                dve.wait_ge(y_turned, n + 1)
                after(dve, mixed_ready, n - 1)
                for c in range(CHUNKS):
                    ins = dve.tensor_copy(y_ch[:, n % 2, c, 1:TOK + 1], turn_ps[:, c * TOK:(c + 1) * TOK])
                ins.then_inc(y_ch_ready, 1)
                dve.wait_ge(edge_ready, n + 1)
                dve.wait_ge(y_ch_ready, n + 1)
                after(dve, mixed_ready, n)
                for w in range(2):
                    for c in range(CHUNKS):
                        ins = dve.tensor_scalar(prev_part[:, w, c, :], y_ch[:, n % 2, c, 0:TOK], mu_c[:, w, c:c + 1],
                                                None, ALU.mult)
                ins.then_inc(prev_ready, 1)

            def mix(n):
                dve.wait_ge(prev_ready, n + 1)
                after(dve, k_ready, n - 1)
                for w in range(2):
                    for c in range(CHUNKS):
                        ins = dve.scalar_tensor_tensor(mixed[:, n % 2, w, c, :], y_ch[:, n % 2, c, 1:TOK + 1],
                                                       mu_s[:, w, c:c + 1], prev_part[:, w, c, :],
                                                       ALU.mult, ALU.add)
                ins.then_inc(mixed_ready, 1)

            def square(n):
                dve.wait_ge(relu_ready, n + 1)
                after(dve, kv_ready, 2 * (n - 1))
                dve.tensor_tensor(key_act[:, n % 2], relu, relu, ALU.mult).then_inc(key_ready, 1)

            def finish(n, half):
                t = slice(2 * half, 2 * half + 2)
                dve.wait_ge(kv_ready, 2 * n + half + 1)
                dve.wait_ge(gate_ready, n + 1)
                dve.tensor_tensor(gated[:, t].rearrange("p t d -> p (t d)"), value_ps[half][:, :],
                                  gate[:, n % 2, t].rearrange("p t d -> p (t d)"), ALU.mult).then_inc(gated_ready, 1)
                dve.wait_ge(gated_ready, 2 * n + half + 1)
                dve.tensor_tensor(z_block(n)[:, t], gated[:, t], y_blk[:, n % 4, t], ALU.add).then_inc(z2_ready, 1)

            def block_stats(n, half):
                dve.wait_ge(z2_ready, 2 * n + half + 1)
                tile_stats(range(n * TPB + 2 * half, n * TPB + 2 * half + 2))

            def period(i, l, first=False, heads_after=2):
                h, _ = head(i, l)
                k = ring_base(h)
                for ops in period_ops(first, heads_after):
                    ring_reads(ops, k, i, l)
                    k = k + ring_len(ops)

            ring_reads(OPENING, 0, -1, STACKS - 1)
            period(-1, STACKS - 1, first=True)
            with dve.Fori(0, LOOPS) as i:
                for l in range(STACKS):
                    period(i, l)
            for l in range(STACKS - 2):
                period(LOOPS, l, heads_after=STACKS - 2 - l)
            dve.wait_ge(c_in, 2 * DMA)
            dve.tensor_scalar(mu_c, mu_s, -1.0, 1.0, ALU.mult, ALU.add).then_inc(c_small, 1)
            dve.wait_ge(z_ready, HEADS)
            tile_stats(range(TILES))
            period(LOOPS, STACKS - 2, heads_after=0)
            dve.wait_ge(rstd_ready, 1)
            dve.wait_ge(c_small, 1)
            normalise(0)
            normalise(1)
            for n in range(EARLY_BLOCKS):
                edge(n)
                take_turned(n)
                if n < 2:
                    mix(n)
                    normalise(n + 2)
            slot_of[0] ^= 1
            ring_reads([("ctx", 0, 0)], RING_TOTAL - 1, LOOPS, STACKS - 2)

            dve.wait_ge(z_ready, ALL_HEADS)
            tile_stats(range(TILES, TILES + TILES // 2))
            square(0)
            tile_stats(range(TILES + TILES // 2, BATCH * TILES))
            for n in range(1, A_GROUPS):
                if n == 2:
                    dve.wait_ge(rstd_ready, 2)
                if 2 <= n and n + 2 < A_GROUPS:
                    normalise(n + 2)
                if n + 1 < A_GROUPS:
                    if n > 1:
                        edge(n + 1)
                    mix(n + 1)
                if n == A_GROUPS - 1:
                    square(n)
                for half in range(2):
                    finish(n - 1, half)
                if n < A_GROUPS - 1:
                    square(n)
                for half in range(2):
                    block_stats(n - 1, half)
            for half in range(2):
                finish(A_GROUPS - 1, half)
                block_stats(A_GROUPS - 1, half)
            for n in range(POOL_OUT, A_GROUPS):
                dve.wait_ge(rstd2_ready, n + 1)
                for tile in range(n * TPB, (n + 1) * TPB):
                    ins = dve.tensor_scalar(z_tile(tile), z_tile(tile), moments[:, tile, 0:1],
                                            rstd2[:, tile:tile + 1], ALU.subtract, ALU.mult)
                ins.then_inc(last_ready, 1)


def rotary_tables():
    inv = np.power(np.float32(10000.0), np.float32(-2.0) * np.arange(PAIRS, dtype=np.float32) / np.float32(HEAD_DIM))
    ang = np.arange(SEQ, dtype=np.float32)[None, :] * inv.astype(np.float32)[:, None]
    return (np.tile(np.cos(ang).astype(np.float32), (HEADS, 1)), np.tile(np.sin(ang).astype(np.float32), (HEADS, 1)))


def kernel(**inputs):
    import concourse.bacc as bacc
    from concourse.bass_utils import run_bass_kernel_spmd
    import ml_dtypes

    x = np.asarray(inputs["L0_attn_hidden_states"]).reshape(BATCH * SEQ, DIM)
    wq, wk, wv = (np.asarray(inputs[f"L0_attn_W{n}"]) for n in "qkv")
    bq, bk, bv = (np.asarray(inputs[f"L0_attn_b{n}"]) for n in "qkv")
    even, odd = np.arange(0, DIM, 2), np.arange(1, DIM, 2)
    cos_t, sin_t = rotary_tables()
    arrays = {
        "x_tok": x,
        "x_ch": np.ascontiguousarray(x.T).reshape(CHUNKS, P, BATCH * SEQ),
        "w_qk": np.concatenate([wq[:, even], wk[:, even], wq[:, odd], wk[:, odd]], axis=1),
        "b_qk": np.stack([bq[even], bk[even], bq[odd], bk[odd]], axis=1),
        "w_v": wv,
        "b_v": bv,
        "w_rkv": np.stack([np.asarray(inputs[f"L0_ffn_W_{n}"]).T for n in "rkv"]),
        "mu": np.stack([np.asarray(inputs[f"L0_ffn_mu_{n}"]).reshape(CHUNKS, P) for n in "rk"]).transpose(2, 0, 1),
        "cos_t": cos_t,
        "sin_t": sin_t,
        "ident": np.eye(P, dtype=np.float32),
        "ident_h": np.eye(P, dtype=ml_dtypes.bfloat16),
    }
    arrays = {n: np.ascontiguousarray(a) for n, a in arrays.items()}
    nc = bacc.Bacc("TRN2", target_bir_lowering=False, num_devices=1)
    args = [nc.dram_tensor(n, a.shape, mybir.dt.from_np(a.dtype), kind="ExternalInput").ap()
            for n, a in arrays.items()]
    out = nc.dram_tensor("out", (BATCH * SEQ, DIM), F32, kind="ExternalOutput").ap()
    build(nc, *args, out)
    r = run_bass_kernel_spmd(nc, [arrays], core_ids=[0])
    return r.results[0]["out"].reshape(BATCH, SEQ, DIM)
```
